# Optimizing a Trainium2 kernel written in Bass

```python
import numpy as np
import jax
import jax.numpy as jnp

def _softmax(x, axis=-1):
    return jax.nn.softmax(x, axis=axis)

def _gelu(x):
    return jax.nn.gelu(x, approximate=True)

def _silu(x):
    return jax.nn.silu(x)

def _sigmoid(x):
    return jax.nn.sigmoid(x)

def _layernorm(x, axis=-1, eps=1e-05):
    m = jnp.mean(x, axis=axis, keepdims=True)
    v = jnp.var(x, axis=axis, keepdims=True)
    return (x - m) / jnp.sqrt(v + eps)

def _scatter_add(tgt, idx, src, axis=0):
    return tgt.at[idx].add(src)

def _segment_sum(src, seg, n):
    return jax.ops.segment_sum(src, seg, n)
kernel_name = 'mk_gnn_preln_d4_gnn_r32_779d95'

def setup_inputs(seed: int=0):
    np.random.seed(seed)
    _w = jnp.asarray

    def _rec_inputs():
        import jax
        import jax.numpy as jnp
        _gk = jax.random.key(seed)
        x = -0.0005121 + 1.001 * jax.random.normal(jax.random.fold_in(_gk, 1), (50000, 64), jnp.float32)
        src = jax.random.randint(jax.random.fold_in(_gk, 2), (50000,), 0, 50000, jnp.int32)
        dst = jnp.minimum((50000 * jax.random.uniform(jax.random.fold_in(_gk, 3), (50000,)) ** 2.0).astype(jnp.int32), 49999)
        _o = jnp.argsort(dst, stable=True)
        src = src[_o]
        dst = dst[_o]
        edge_attr_3 = 0.000669165 + 0.999965 * jax.random.normal(jax.random.fold_in(_gk, 12), (50000, 3), jnp.float32)
        return (x, src, dst, edge_attr_3)
    x, src, dst, edge_attr_3 = _rec_inputs()

    def _L0_gnn_setup():
        import jax, jax.numpy as jnp
        import numpy as np
        N = 50000
        E = 25000
        D_IN = 64
        D_OUT = 64
        key = jax.random.key(seed)
        k1, k2, k3 = jax.random.split(key, 3)
        x = jax.random.normal(k1, (N, D_IN), dtype=jnp.float32)
        edge_index = jax.random.randint(k2, (2, E), 0, N, dtype=jnp.int32)
        W = jax.random.normal(k3, (D_OUT, D_IN), dtype=jnp.float32) * 0.05
        b = jnp.zeros((D_OUT,), dtype=jnp.float32)
        prelu_a = jnp.full((1,), 0.25, dtype=jnp.float32)
        return {'x': x, 'edge_index': edge_index, 'W': W, 'b': b, 'prelu_a': prelu_a}
    _L0_gnn_all = _L0_gnn_setup()
    _L0_gnn_in = {k: v for k, v in _L0_gnn_all.items() if k in ('W', 'b', 'prelu_a')}
    del _L0_gnn_all

    def _L1_gnn_setup():
        import jax, jax.numpy as jnp
        import numpy as np
        N_NODES = 50000
        N_EDGES = 25000
        D_IN = 64
        D_OUT = 64
        key = jax.random.key(seed)
        k1, k2, k3 = jax.random.split(key, 3)
        x = jax.random.normal(k1, (N_NODES, D_IN), dtype=jnp.float32)
        edge_index = jax.random.randint(k2, (2, N_EDGES), 0, N_NODES, dtype=jnp.int64)
        limit = np.sqrt(6.0 / (D_IN + D_OUT)).astype(np.float32)
        weight = jax.random.uniform(k3, (D_IN, D_OUT), dtype=jnp.float32, minval=-limit, maxval=limit)
        bias = jnp.zeros((D_OUT,), dtype=jnp.float32)
        return {'x': x, 'edge_index': edge_index, 'weight': weight, 'bias': bias}
    _L1_gnn_all = _L1_gnn_setup()
    _L1_gnn_in = {k: v for k, v in _L1_gnn_all.items() if k in ('weight', 'bias')}
    del _L1_gnn_all

    def _L2_gnn_setup():
        import jax, jax.numpy as jnp
        import numpy as np
        N_NODES = 50000
        N_EDGES = 25000
        IN_NF = 64
        HID_NF = 64
        OUT_NF = 64

        def _linear_init(key, fan_in, fan_out):
            kw, kb = jax.random.split(key)
            bound = 1.0 / np.sqrt(fan_in)
            W = jax.random.uniform(kw, (fan_in, fan_out), jnp.float32, -bound, bound)
            b = jax.random.uniform(kb, (fan_out,), jnp.float32, -bound, bound)
            return (W, b)
        key = jax.random.key(seed)
        ks = jax.random.split(key, 9)
        h = jax.random.normal(ks[0], (N_NODES, IN_NF), jnp.float32)
        edges_index = jax.random.randint(ks[1], (2, N_EDGES), 0, N_NODES, jnp.int64)
        coord_diff = jax.random.normal(ks[2], (N_EDGES, 3), jnp.float32)
        We1, be1 = _linear_init(ks[3], 2 * IN_NF + 1, HID_NF)
        We2, be2 = _linear_init(ks[4], HID_NF, HID_NF)
        Wa, ba = _linear_init(ks[5], HID_NF, 1)
        Wn1, bn1 = _linear_init(ks[6], HID_NF + IN_NF, HID_NF)
        Wn2, bn2 = _linear_init(ks[7], HID_NF, OUT_NF)
        return {'h': h, 'edges_index': edges_index, 'coord_diff': coord_diff, 'We1': We1, 'be1': be1, 'We2': We2, 'be2': be2, 'Wa': Wa, 'ba': ba, 'Wn1': Wn1, 'bn1': bn1, 'Wn2': Wn2, 'bn2': bn2}
    _L2_gnn_all = _L2_gnn_setup()
    _L2_gnn_in = {k: v for k, v in _L2_gnn_all.items() if k in ('We1', 'be1', 'We2', 'be2', 'Wa', 'ba', 'Wn1', 'bn1', 'Wn2', 'bn2')}
    del _L2_gnn_all

    def _L3_gnn_setup():
        import jax, jax.numpy as jnp
        import numpy as np
        N_NODES = 3125
        N_EDGES = 31250
        D_IN = 64
        D_OUT = 64
        key = jax.random.key(seed)
        k_x, k_e, k_w, k_b = jax.random.split(key, 4)
        x = jax.random.normal(k_x, (N_NODES, D_IN), dtype=jnp.float32)
        edge_index = jax.random.randint(k_e, (2, N_EDGES), 0, N_NODES, dtype=jnp.int64)
        deg = jax.ops.segment_sum(jnp.ones((N_EDGES,), jnp.float32), edge_index[1], num_segments=N_NODES)
        node_degrees = jnp.maximum(deg, 1.0)
        W = jax.random.normal(k_w, (D_OUT, D_IN), dtype=jnp.float32) * (1.0 / np.sqrt(D_IN))
        b = jax.random.normal(k_b, (D_OUT,), dtype=jnp.float32) * 0.01
        return {'x': x, 'edge_index': edge_index, 'node_degrees': node_degrees, 'W': W, 'b': b}
    _L3_gnn_all = _L3_gnn_setup()
    _L3_gnn_in = {k: v for k, v in _L3_gnn_all.items() if k in ('W', 'b')}
    del _L3_gnn_all
    return {'x': x, 'src': src, 'dst': dst, 'edge_attr_3': edge_attr_3, 'L0_gnn_W': _L0_gnn_in['W'], 'L0_gnn_b': _L0_gnn_in['b'], 'L0_gnn_prelu_a': _L0_gnn_in['prelu_a'], 'L1_gnn_weight': _L1_gnn_in['weight'], 'L1_gnn_bias': _L1_gnn_in['bias'], 'L2_gnn_We1': _L2_gnn_in['We1'], 'L2_gnn_be1': _L2_gnn_in['be1'], 'L2_gnn_We2': _L2_gnn_in['We2'], 'L2_gnn_be2': _L2_gnn_in['be2'], 'L2_gnn_Wa': _L2_gnn_in['Wa'], 'L2_gnn_ba': _L2_gnn_in['ba'], 'L2_gnn_Wn1': _L2_gnn_in['Wn1'], 'L2_gnn_bn1': _L2_gnn_in['bn1'], 'L2_gnn_Wn2': _L2_gnn_in['Wn2'], 'L2_gnn_bn2': _L2_gnn_in['bn2'], 'L3_gnn_W': _L3_gnn_in['W'], 'L3_gnn_b': _L3_gnn_in['b']}

def reference(x, src, dst, edge_attr_3, L0_gnn_W, L0_gnn_b, L0_gnn_prelu_a, L1_gnn_weight, L1_gnn_bias, L2_gnn_We1, L2_gnn_be1, L2_gnn_We2, L2_gnn_be2, L2_gnn_Wa, L2_gnn_ba, L2_gnn_Wn1, L2_gnn_bn1, L2_gnn_Wn2, L2_gnn_bn2, L3_gnn_W, L3_gnn_b):
    import jax
    import jax.numpy as jnp

    def _L0_gnn_ref(x, edge_index, W, b, prelu_a):
        import jax, jax.numpy as jnp
        import numpy as np
        N = 50000
        E = 25000
        D_IN = 64
        D_OUT = 64
        n = x.shape[0]
        row, col = (edge_index[0], edge_index[1])
        loop = jnp.arange(n, dtype=edge_index.dtype)
        row = jnp.concatenate([row, loop])
        col = jnp.concatenate([col, loop])
        ones = jnp.ones(row.shape[0], dtype=x.dtype)
        deg = jax.ops.segment_sum(ones, col, num_segments=n)
        dinv = jnp.where(deg > 0, jax.lax.rsqrt(deg), 0.0)
        norm = dinv[row] * dinv[col]
        h = x @ W.T
        msg = h[row] * norm[:, None]
        out = jax.ops.segment_sum(msg, col, num_segments=n) + b
        return jnp.where(out >= 0, out, prelu_a * out)

    def _L1_gnn_ref(x, edge_index, weight, bias):
        import jax, jax.numpy as jnp
        import numpy as np
        N_NODES = 50000
        N_EDGES = 25000
        D_IN = 64
        D_OUT = 64
        n = x.shape[0]
        loops = jnp.arange(n, dtype=edge_index.dtype)
        row = jnp.concatenate([edge_index[0], loops])
        col = jnp.concatenate([edge_index[1], loops])
        deg = jax.ops.segment_sum(jnp.ones_like(row, dtype=x.dtype), row, num_segments=n)
        deg_inv_sqrt = jnp.where(deg > 0, jax.lax.rsqrt(deg), jnp.zeros_like(deg))
        norm = deg_inv_sqrt[row] * deg_inv_sqrt[col]
        h = x @ weight
        out = jax.ops.segment_sum(h[row] * norm[:, None], col, num_segments=n)
        return out + bias

    def _L2_gnn_ref(h, edges_index, coord_diff, We1, be1, We2, be2, Wa, ba, Wn1, bn1, Wn2, bn2):
        import jax, jax.numpy as jnp
        import numpy as np
        N_NODES = 50000
        N_EDGES = 25000
        IN_NF = 64
        HID_NF = 64
        OUT_NF = 64

        def _linear_init(key, fan_in, fan_out):
            kw, kb = jax.random.split(key)
            bound = 1.0 / np.sqrt(fan_in)
            W = jax.random.uniform(kw, (fan_in, fan_out), jnp.float32, -bound, bound)
            b = jax.random.uniform(kb, (fan_out,), jnp.float32, -bound, bound)
            return (W, b)
        row = edges_index[0]
        col = edges_index[1]
        radial = jnp.sum(coord_diff ** 2, axis=1, keepdims=True)
        edge_in = jnp.concatenate([h[row], h[col], radial], axis=1)
        e = jax.nn.silu(edge_in @ We1 + be1)
        e = jax.nn.silu(e @ We2 + be2)
        att = jax.nn.sigmoid(e @ Wa + ba)
        e = e * att
        agg = jax.ops.segment_sum(e, row, num_segments=h.shape[0])
        node_in = jnp.concatenate([h, agg], axis=1)
        out = jax.nn.silu(node_in @ Wn1 + bn1) @ Wn2 + bn2
        return out

    def _L3_gnn_ref(x, edge_index, node_degrees, W, b):
        import jax, jax.numpy as jnp
        import numpy as np
        N_NODES = 3125
        N_EDGES = 31250
        D_IN = 64
        D_OUT = 64
        src, dst = (edge_index[0], edge_index[1])
        agg = jax.ops.segment_sum(x[src], dst, num_segments=x.shape[0])
        mean = agg / node_degrees[:, None]
        return mean @ W.T + b
    edge_index = jnp.stack([src, dst])
    deg = jnp.maximum(jax.ops.segment_sum(jnp.ones(dst.shape, jnp.float32), dst, num_segments=50000), 1.0)
    h = jnp.maximum(_layernorm(x, axis=-1), 0.0)
    x = x + _L0_gnn_ref(h, edge_index, L0_gnn_W, L0_gnn_b, L0_gnn_prelu_a)
    h = jnp.maximum(_layernorm(x, axis=-1), 0.0)
    x = x + _L1_gnn_ref(h, edge_index, L1_gnn_weight, L1_gnn_bias)
    h = jnp.maximum(_layernorm(x, axis=-1), 0.0)
    x = x + _L2_gnn_ref(h, edge_index, edge_attr_3, L2_gnn_We1, L2_gnn_be1, L2_gnn_We2, L2_gnn_be2, L2_gnn_Wa, L2_gnn_ba, L2_gnn_Wn1, L2_gnn_bn1, L2_gnn_Wn2, L2_gnn_bn2)
    h = jnp.maximum(_layernorm(x, axis=-1), 0.0)
    x = x + _L3_gnn_ref(h, edge_index, deg, L3_gnn_W, L3_gnn_b)
    return x

_drawn_inputs = setup_inputs


def setup_inputs(seed=0):
    import zlib

    import numpy as np

    out = dict(_drawn_inputs(seed))
    spreads = {'L0_gnn_b': (0.0, 0.1), 'L1_gnn_bias': (0.0, 0.1)}
    factors = {'edge_attr_3': 8.0,
     'L2_gnn_We1': 8.0,
     'L2_gnn_be1': 26.549,
     'L2_gnn_We2': 8.0,
     'L2_gnn_be2': 25.112,
     'L2_gnn_Wa': 8.0,
     'L2_gnn_bn1': 4.45,
     'L3_gnn_b': 6.66}
    for name, (base, spread) in spreads.items():
        noise = np.random.default_rng([zlib.crc32(name.encode()), seed]).standard_normal(out[name].shape)
        drawn = base * np.exp(spread * noise) if base else spread * noise
        out[name] = jnp.asarray(drawn.astype(out[name].dtype))
    for name, factor in factors.items():
        out[name] = (out[name] * factor).astype(out[name].dtype)
    return out
```

```python
from contextlib import ExitStack

import concourse.bass as bass
from concourse import mybir

F32 = mybir.dt.float32
F16 = mybir.dt.float16
I32 = mybir.dt.int32
ALU = mybir.AluOpType
ACT = mybir.ActivationFunctionType
AX = mybir.AxisListType

P = 128
N = 50000
E = 50000
D = 64
C = 392
FULL = N // C
REST = N - FULL * C
ROWS = P * C
DUMP = ROWS
EPS = 1e-5

PAIRS = C // 2
RING = 7
CHUNK = 14
CHUNKS = C // CHUNK
CW = CHUNK * D
NRING = 2
ZW = CW // 2
W2 = 2 * D

L0, L1, L2, L3 = range(4)


def wait(eng, sem, value):
    if not (isinstance(value, int) and value <= 0):
        eng.wait_ge(sem, value)


def pipeline(eng, steps, ring, stages):
    for s in range(ring):
        for lag, stage in stages:
            if s >= lag:
                stage(s - lag, s - lag, 0)
    with eng.Fori(1, steps // ring) as i:
        for s in range(ring):
            for lag, stage in stages:
                stage(i * ring + (s - lag), (s - lag) % ring, i + (s - lag) // ring)
    for s in range(max(lag for lag, _ in stages)):
        for lag, stage in stages:
            if s < lag:
                stage(steps + s - lag, (s - lag) % ring, steps // ring + (s - lag) // ring)


def linker(eng, sem, before):
    count = [before]

    def link(ins):
        count[0] = count[0] + 1
        ins.then_inc(sem, 1)
        eng.wait_ge(sem, count[0])
    return link


def gnn_kernel(nc, x, src, dst, edge_attr, W0, b0, prelu_a, W1, b1, We1, be1, We2, be2, Wa, ba,
               Wn1, bn1, Wn2, bn2, W3, b3, out):
    table = [nc.dram_tensor(f"table{l}", [ROWS, D], F32, kind="Internal").ap() for l in range(4)]
    acc = [[nc.dram_tensor(f"acc{l}_{k}", [ROWS + P, D], F32, kind="Internal").ap() for k in range(2)]
           for l in range(4)]

    def by_partition(t):
        return t[0:ROWS, :].rearrange("(p t) d -> p (t d)", p=P)

    with ExitStack() as ctx:
        def sb(name, shape, dt=F32):
            return ctx.enter_context(nc.sbuf_tensor(name, shape, dt))

        def sem(name):
            return ctx.enter_context(nc.semaphore(name))

        xr = sb("x_resident", [P, C * D])
        index = [sb("dst_index", [P, C], I32), sb("src_index", [P, C], I32)]
        meta = [sb(f"meta{k}", [P, C, 3]) for k in range(2)]
        scatter = [sb(f"scatter{k}", [P, C], I32) for k in range(2)]
        rank = sb("rank", [P, C])
        dinv = [sb(f"dinv{k}", [P, C]) for k in range(2)]
        rdeg = sb("rdeg", [P, C])
        radial = sb("radial", [P, C])
        colf = sb("colf", [P, P])
        col16 = sb("col16", [P, C], F16)
        pcol = sb("pcol", [P, 1])
        dumprow = sb("dumprow", [P, 1])
        tri = sb("tri", [P, P])
        zero = sb("zero", [P, ZW])
        expo = sb("exponent", [P, 1])
        ext = sb("ident_wa", [P, P + 2])
        ident = ext[:, 0:P]
        mats = ("W0", "W1", "W3", "We1s", "We1d", "We2", "Wn1h", "Wn1a", "Wn2")
        bd = {n: sb(f"bd_{n}", [P, P]) for n in mats}
        wrad = sb("w_radial", [P, D])
        bias = [sb(f"bias{l}", [P, D]) for l in range(4)]
        be1c, be2c, bn1c, bac, alpha, nalpha = (sb(n, [P, 1]) for n in
                                                ("be1c", "be2c", "bn1c", "bac", "alpha", "nalpha"))

        ARENA = 12 * CW + 1400
        arena = sb("arena", [P, ARENA])
        used = [0]

        def part(n):
            used[0] += n
            assert used[0] <= ARENA, used[0]
            return arena[:, used[0] - n:used[0]]

        e_int = [part(4).bitcast(I32) for _ in range(RING)]
        e_sct = [part(2).bitcast(I32) for _ in range(RING)]
        e_flt = [part(4) for _ in range(RING)]
        e_meta = [part(6) for _ in range(RING)]
        e_rank = [part(2) for _ in range(RING)]
        e_att = [part(2) for _ in range(RING)]
        e_row = [[part(W2) for _ in range(RING)] for _ in range(2)]
        e_msg = [part(W2) for _ in range(RING)]
        e_eq = [part(2 * P) for _ in range(RING)]
        e_raw = [part(W2) for _ in range(RING)]
        e_T = [part(2 * P) for _ in range(2)]
        e_X = [part(W2) for _ in range(RING)]
        e_sig1 = [part(P) for _ in range(2)]
        e_sig2 = [part(P) for _ in range(2)]
        e_h1 = [part(P) for _ in range(2)]
        e_h2 = [part(P) for _ in range(2)]
        hot = part(P + C).bitcast(F16)
        junk = [[part(P) for _ in range(2)] for _ in range(2)]
        edge_used = used[0]
        attr = part(3 * C)
        tmp = [part(C) for _ in range(4)]
        tmpi = part(C).bitcast(I32)
        used[0] = 0
        n_a = [[part(CW) for _ in range(NRING)] for _ in range(2)]
        n_b, n_T, n_y, n_r, n_q, n_s = (part(CW) for _ in range(6))
        n_h = [part(CW) for _ in range(NRING)]
        n_m, n_v = part(CHUNK), part(CHUNK)

        psum = ctx.enter_context(nc.psum_tensor("psum", [P, 8, 512], F32))
        p_hist = psum[:, 0, 0:C]
        p_key = [psum[:, 1 + k, :] for k in range(2)]
        p_sum = [psum[:, 3 + k, 0:W2] for k in range(2)]
        p_T = psum[:, 5, 0:2 * P]
        p_mlp = [psum[:, 6, 0:P], psum[:, 7, 0:P]]
        p_nat = psum[:, 0, 0:P + 2]
        flat = psum[:, :, :].rearrange("p b c -> p (b c)")
        p_nT = [flat[:, 2048 * 0 + 1024 * k:1024 * k + CW] for k in range(2)]
        p_nO = [flat[:, 2048 + 1024 * k:2048 + 1024 * k + CW] for k in range(2)]

        x_loaded, edges_loaded, weights_loaded = sem("x_loaded"), sem("edges_loaded"), sem("weights_loaded")
        pad_clear, iota_done, setup_step, setup_pow = (sem(n) for n in
                                                       ("pad_clear", "iota_done", "setup_step", "setup_pow"))
        zero_ready, zeroed = sem("zero_ready"), sem("zeroed")
        flipped, flip_copied = sem("flipped"), sem("flip_copied")
        squares = sem("attr_squares")
        hist_open, meta_ready, keys_spread, ranked = (sem(n) for n in
                                                      ("hist_open", "meta_ready", "keys_spread", "ranked"))
        onehot, counted, rank_kept = sem("onehot"), sem("counted"), sem("rank_kept")
        rows_ready = sem("rows_ready")
        gathered = [sem(f"gathered{s}") for s in range(RING)]
        key_spread, equal, summed, msg_ready = (sem(n) for n in ("key_spread", "equal", "summed", "msg_ready"))
        added = [sem(f"added{k}") for k in range(2)]
        flipped_rows, rows_T, radial_term = sem("flipped_rows"), sem("rows_T"), sem("radial_term")
        mlp1, sig1, act1, mlp2, sig2, act2 = (sem(n) for n in ("mlp1", "sig1", "act1", "mlp2", "sig2", "act2"))
        natural, att_ready, weighted = sem("natural"), sem("att_ready"), sem("weighted")
        loaded = [sem(f"loaded{k}") for k in range(NRING)]
        agg_T, agg_T_kept, agg_out = sem("agg_T"), sem("agg_T_kept"), sem("agg_out")
        z_out, z_sig, z_ready = sem("z_out"), sem("z_sig"), sem("z_ready")
        o_read, biased, rectified, x_new = sem("o_read"), sem("biased"), sem("rectified"), sem("x_new")
        post_step, ln_step = sem("post_step"), sem("ln_step")
        centred, squared, var_ready, rstd_ready, h_ready = (sem(n) for n in
                                                            ("centred", "squared", "var_ready", "rstd_ready", "h_ready"))
        stored = [sem(f"stored{k}") for k in range(NRING)]
        out_stored = sem("out_stored")

        sources = [[], [acc[0][0], acc[0][1]], [acc[1][0], acc[1][1]], [acc[2][0], acc[2][1], table[2]],
                   [acc[3][0], acc[3][1]]]
        targets = [[table[0], acc[0][0]], [table[1], acc[1][0]], [table[2]], [table[3]]]
        HALF = CHUNKS // NRING
        loads_before = [16 * HALF * sum(len(s) for s in sources[:n]) for n in range(6)]
        stores_before = [16 * HALF * sum(len(t) for t in targets[:n]) for n in range(5)]

        finalised, counts_plus, hist_closed = sem("finalised"), sem("counts_plus"), sem("hist_closed")
        wait_over, wait_over_v = sem("wait_over"), sem("wait_over_v")
        meta_built, weights_clear, x_new1, scaled = (sem(n) for n in
                                                    ("meta_built", "weights_clear", "x_new1", "scaled"))
        parts = ((0, 96), (96, 112), (112, FULL))

        def filled(a, w):
            return a[0:FULL * C, :].rearrange("(p t) d -> p (t d)", t=C)

        def rest(a):
            return a[FULL * C:N, :].rearrange("(p t) d -> p (t d)", p=1)

        def pair(t, j):
            return t[:, j * W2:(j + 1) * W2]

        def cols(c):
            return bass.ds(c * CHUNK, CHUNK)

        def spread(t, n):
            return t.unsqueeze(2).to_broadcast([P, n, D])

        def grid(t, n=CHUNK):
            return t.rearrange("p (t d) -> p t d", d=D) if len(t.shape) == 2 else t

        def x_of(c):
            return xr[:, bass.ds(c * CW, CW)]

        def last_use(q, slot):
            return q if slot == 0 else q - 1

        def key_of(l):
            return 1 if l == L2 else 0

        tables_in = [1, 1, 2, 1]
        gathers_before = [16 * 2 * (PAIRS // RING) * sum(tables_in[:l]) for l in range(4)]
        Z_FIRST = C * D // ZW
        ZERO0 = 16 * (Z_FIRST + 3)
        ZERO_ALL = ZERO0 + 16 * 5 * (Z_FIRST + 1)
        EDGE_LOADS = 16 * 4 * 3
        WEIGHT_LOADS = 16 * (2 * len(mats) + 2 + 1 + 4 + 6 + 2)

        block = ctx.enter_context(nc.Block())

        @block.sync
        def _(sp):
            src2, dst2 = (a.rearrange("(n o) -> n o", o=1) for a in (src, dst))
            todo = [(attr, edge_attr, 3), (index[0], dst2, 1), (index[1], src2, 1)]
            for tile, a, w in todo:
                sp.dma_start(tile[0:96, :], filled(a, w)[0:96, :]).then_inc(edges_loaded, 16)
            sp.dma_start(xr[0:96, :], filled(x, D)[0:96, :]).then_inc(x_loaded, 16)
            sp.wait_ge(pad_clear, 1)
            for tile, a, w in todo:
                for lo, hi in parts[1:]:
                    sp.dma_start(tile[lo:hi, :], filled(a, w)[lo:hi, :]).then_inc(edges_loaded, 16)
                sp.dma_start(tile[FULL:P, 0:REST * w], rest(a)).then_inc(edges_loaded, 16)
            for lo, hi in parts[1:]:
                sp.dma_start(xr[lo:hi, :], filled(x, D)[lo:hi, :]).then_inc(x_loaded, 16)
            sp.dma_start(xr[FULL:P, 0:REST * D], rest(x)).then_inc(x_loaded, 16)

            def clear(a):
                with sp.Fori(0, Z_FIRST) as i:
                    sp.dma_start(by_partition(a)[:, bass.ds(i * ZW, ZW)], zero[:, :]).then_inc(zeroed, 16)

            def clear_spare(a):
                sp.dma_start(a[DUMP:DUMP + P, :], zero[:, 0:D]).then_inc(zeroed, 16)

            sp.wait_ge(zero_ready, 1)
            clear(acc[0][1])
            for a in (acc[0][0], acc[0][1], acc[1][0]):
                clear_spare(a)

            for n in range(5):
                if n == 1:
                    for a in (acc[1][1], acc[2][0], acc[2][1], acc[3][0], acc[3][1]):
                        clear(a)
                        clear_spare(a)
                    sp.wait_ge(finalised, 2)
                if n:
                    for k in range(2):
                        sp.wait_ge(added[k], 16 * PAIRS * n)

                def load(c, slot, turn, n=n):
                    wait(sp, agg_T, (n - 1) * CHUNKS + c - (0 if n == 3 else 1))
                    for buf, a in zip((n_a[0][slot], n_a[1][slot], n_b), sources[n]):
                        sp.dma_start(buf, by_partition(a)[:, bass.ds(c * CW, CW)]).then_inc(loaded[slot], 16)

                def store(c, slot, turn, n=n):
                    sp.wait_ge(h_ready, n * CHUNKS + c + 1)
                    for a in targets[n]:
                        sp.dma_start(by_partition(a)[:, bass.ds(c * CW, CW)], n_h[slot]).then_inc(stored[slot], 16)

                def store_out(c, slot, turn):
                    sp.wait_ge(x_new, c + 1)
                    for lo, hi in ((0, 112), (112, FULL)):
                        sp.dma_start(filled(out, D)[lo:hi, bass.ds(c * CW, CW)],
                                     xr[lo:hi, bass.ds(c * CW, CW)]).then_inc(out_stored, 16)

                stages = [(0, load)] if n else []
                stages.append((2, store if n < 4 else store_out))
                pipeline(sp, CHUNKS, NRING, stages)
            sp.dma_start(rest(out), xr[FULL:P, 0:REST * D]).then_inc(out_stored, 16)
            sp.wait_ge(out_stored, 16 * (2 * CHUNKS + 1))

        @block.gpsimd
        def _(pool):
            nc.gpsimd.iota(tmpi, [[1, C]], base=0, channel_multiplier=0).then_inc(iota_done, 1)
            pool.wait_ge(setup_step, 1)
            nc.gpsimd.iota(tmpi, [[1, C]], base=0, channel_multiplier=C).then_inc(iota_done, 1)
            nc.gpsimd.iota(e_int[0][:, 0:1], [[0, 1]], base=0, channel_multiplier=1)
            nc.gpsimd.iota(e_int[0][:, 1:2], [[0, 1]], base=DUMP, channel_multiplier=1)
            nc.gpsimd.memset(expo[:, :], -0.5).then_inc(iota_done, 1)

            def power(t, k):
                pool.wait_ge(counts_plus, k + 1)
                nc.gpsimd.tensor_tensor(t[:, :], t[:, :], expo[:, 0:1].to_broadcast([P, C]),
                                        ALU.pow).then_inc(setup_pow, 1)

            power(dinv[0], 0)
            for n in range(5):
                if n < 4:
                    def rstd(c, slot, turn, n=n):
                        pool.wait_ge(var_ready, n * CHUNKS + c + 1)
                        nc.gpsimd.tensor_tensor(n_v, n_v, expo[:, 0:1].to_broadcast([P, CHUNK]),
                                                ALU.pow).then_inc(rstd_ready, 1)
                    pipeline(pool, CHUNKS, NRING, [(0, rstd)])
                    l = n

                    def gather(q, slot, turn, l=l):
                        pool.wait_ge(rows_ready, l * PAIRS + q + 1)
                        pool.sem_inc(wait_over, 1)
                        for k in range(tables_in[l]):
                            for j in range(2):
                                nc.gpsimd.indirect_dma_start(
                                    out=e_row[k][slot][:, j * D:(j + 1) * D], out_offset=None, in_=table[l][:, :],
                                    in_offset=bass.IndirectOffsetOnAxis(
                                        ap=e_int[slot][:, 2 * k + j:2 * k + j + 1], axis=0),
                                ).then_inc(gathered[slot], 16)

                    def add(q, slot, turn, l=l):
                        pool.wait_ge(msg_ready, l * PAIRS + q + 1)
                        for j in range(2):
                            wait(pool, added[j], 16 * (l * PAIRS + q))
                            pool.sem_inc(wait_over, 1)
                            nc.gpsimd.indirect_dma_start(
                                out=acc[l][j][:, :],
                                out_offset=bass.IndirectOffsetOnAxis(ap=e_sct[slot][:, j:j + 1], axis=0),
                                in_=e_msg[slot][:, j * D:(j + 1) * D], in_offset=None,
                                compute_op=ALU.add).then_inc(added[j], 16)

                    pool.wait_ge(zeroed, ZERO0 if l == 0 else ZERO_ALL)
                    pipeline(pool, PAIRS, RING, [(0, gather), (4 if l == L2 else 3, add)])
                    if l == 0:
                        power(dinv[1], 1)

        @block.scalar
        def _(act):
            def load(dst_, src_):
                act.dma_start(dst_, src_).then_inc(weights_loaded, 16)

            act.wait_ge(weights_clear, 1)
            blocks = {"W0": W0, "W1": W1, "W3": W3, "We1s": We1[0:D, :], "We1d": We1[D:2 * D, :], "We2": We2,
                      "Wn1h": Wn1[D - D:D, :], "Wn1a": Wn1[D:2 * D, :], "Wn2": Wn2}
            for name in mats:
                for h in range(2):
                    load(bd[name][h * D:(h + 1) * D, h * D:(h + 1) * D], blocks[name])
            for h in range(2):
                load(ext[h * D:(h + 1) * D, P + h:P + h + 1], Wa)
            load(wrad[:, :], We1[2 * D:2 * D + 1, :].to_broadcast([P, D]))
            for l, b in enumerate((b0, b1, bn2, b3)):
                load(bias[l][:, :], b.rearrange("(o d) -> o d", o=1).to_broadcast([P, D]))
            for t, b in ((be1c, be1), (be2c, be2), (bn1c, bn1)):
                for h in range(2):
                    load(t[h * D:(h + 1) * D, :], b.rearrange("(d o) -> d o", o=1))
            for t, b in ((bac, ba), (alpha, prelu_a)):
                load(t[:, :], b.rearrange("(o d) -> o d", o=1).to_broadcast([P, 1]))
            act.wait_ge(edges_loaded, EDGE_LOADS)
            nc.scalar.activation(attr, attr, ACT.Square).then_inc(squares, 1)

            def index_load(k):
                def stage(q, slot, turn):
                    wait(act, counted, k * PAIRS + q - RING + 1)
                    nc.scalar.copy(e_meta[slot].rearrange("p (a b) -> p a b", b=3),
                                   meta[k][:, bass.ds(2 * q, 2), :]).then_inc(meta_ready, 1)
                return stage

            def rank_keep(k):
                def stage(q, slot, turn):
                    act.wait_ge(ranked, k * PAIRS + q + 1)
                    nc.scalar.copy(rank[:, bass.ds(2 * q, 2)], e_rank[slot]).then_inc(rank_kept, 1)
                return stage

            act.wait_ge(meta_built, 1)
            pipeline(act, PAIRS, RING, [(0, index_load(0)), (1, rank_keep(0))])

            for n in range(5):
                def keep_T(c, slot, turn, n=n):
                    g = (n - 1) * CHUNKS + c
                    act.wait_ge(agg_T, g + 1)
                    wait(act, agg_out, g)
                    last = nc.scalar.copy(n_T, p_nT[0 if n == 3 else slot])
                    if n == 3:
                        last = nc.scalar.copy(n_y, p_nT[1])
                    last.then_inc(agg_T_kept, 1)

                def rectify(c, slot, turn):
                    act.wait_ge(biased, c + 1)
                    nc.scalar.activation(n_r, n_y, ACT.Relu, scale=-1.0)
                    nc.scalar.activation(n_y, n_y, ACT.Relu).then_inc(rectified, 1)

                def z_sigmoid(c, slot, turn):
                    act.wait_ge(z_out, c + 1)
                    nc.scalar.activation(n_r, p_nO[0], ACT.Sigmoid, bias=bn1c[:, 0:1]).then_inc(z_sig, 1)

                def square(c, slot, turn, n=n):
                    act.wait_ge(centred, n * CHUNKS + c + 1)
                    nc.scalar.activation(n_s, n_q, ACT.Square).then_inc(squared, 1)

                stages = []
                if n == 3:
                    stages.append((1, z_sigmoid))
                if n:
                    stages.append((0, keep_T))
                if n == 1:
                    stages.append((1, rectify))
                if n < 4:
                    stages.append((1, square))
                pipeline(act, CHUNKS, NRING, stages)
                if n == 4:
                    break

                l, k = n, key_of(n)
                for s in range(NRING):
                    act.wait_ge(stored[s], stores_before[l + 1])

                def rows(q, slot, turn, l=l, k=k):
                    for j in range(2):
                        wait(act, added[j], 16 * (l * PAIRS + q - RING + 1))
                    two = bass.ds(2 * q, 2)
                    nc.scalar.copy(e_int[slot][:, 0:2], index[1][:, two])
                    if l == L2:
                        nc.scalar.copy(e_int[slot][:, 2:4], index[0][:, two])
                        nc.scalar.copy(e_flt[slot][:, 2:4], radial[:, two])
                    nc.scalar.copy(e_sct[slot], scatter[k][:, two])
                    nc.scalar.copy(e_flt[slot][:, 0:2], meta[k][:, two, 0]).then_inc(rows_ready, 1)

                def message(q, slot, turn, l=l):
                    act.wait_ge(summed, l * PAIRS + q + 1)
                    nc.scalar.copy(e_msg[slot], p_sum[slot % 2]).then_inc(msg_ready, 1)

                def keep_rows_T(q, slot, turn):
                    act.wait_ge(flipped_rows, q + 1)
                    wait(act, mlp1, last_use(q, slot))
                    nc.scalar.copy(e_T[slot % 2], p_T).then_inc(rows_T, 1)

                def sigmoid1(q, slot, turn):
                    act.wait_ge(mlp1, q + 1)
                    wait(act, act1, last_use(q, slot))
                    nc.scalar.activation(e_sig1[slot % 2], p_mlp[0], ACT.Sigmoid,
                                         bias=be1c[:, 0:1]).then_inc(sig1, 1)

                def sigmoid2(q, slot, turn):
                    act.wait_ge(mlp2, q + 1)
                    wait(act, act2, last_use(q, slot))
                    nc.scalar.activation(e_sig2[slot % 2], p_mlp[1], ACT.Sigmoid,
                                         bias=be2c[:, 0:1]).then_inc(sig2, 1)

                def attention(q, slot, turn):
                    act.wait_ge(natural, q + 1)
                    nc.scalar.activation(e_att[slot], p_nat[:, P:P + 2], ACT.Sigmoid,
                                         bias=bac[:, 0:1]).then_inc(att_ready, 1)

                if l == L2:
                    pipeline(act, PAIRS, RING, [(0, rows), (2, keep_rows_T), (3, sigmoid2), (2, sigmoid1),
                                                (3, attention), (3, message)])
                elif l == L0:
                    pipeline(act, PAIRS, RING, [(0, rows), (0, index_load(1)), (2, rank_keep(1)), (2, message)])
                else:
                    pipeline(act, PAIRS, RING, [(0, rows), (2, message)])

        @block.vector
        def _(dve):
            nc.vector.memset(xr[96:P, REST * D:], 0.0)
            for t, w in ((attr, 3), (index[0], 1), (index[1], 1)):
                last = nc.vector.memset(t[96:P, REST * w:], 0)
            last.then_inc(pad_clear, 1)
            for name in mats:
                nc.vector.memset(bd[name][:, :], 0.0)
            nc.vector.memset(ext[:, P:P + 2], 0.0).then_inc(weights_clear, 1)
            nc.vector.memset(zero[:, :], 0.0).then_inc(zero_ready, 1)

            link = linker(dve, setup_step, 0)
            dve.wait_ge(iota_done, 1)
            link(nc.vector.tensor_copy(tmp[0], tmpi))
            nc.vector.tensor_copy(colf[:, :], tmp[0][:, 0:P])
            link(nc.vector.tensor_copy(col16[:, :], tmp[0]))
            dve.wait_ge(iota_done, 3)
            link(nc.vector.tensor_copy(pcol[:, :], e_int[0][:, 0:1]))
            link(nc.vector.tensor_copy(dumprow[:, :], e_int[0][:, 1:2]))
            nc.vector.tensor_scalar(ident, colf[:, :], pcol[:, 0:1], None, ALU.is_equal)
            nc.vector.tensor_scalar(tri[:, :], colf[:, :], pcol[:, 0:1], None, ALU.is_lt)
            pad = tmp[3]
            link(nc.vector.tensor_copy(pad, tmpi))
            link(nc.vector.tensor_scalar(pad, pad, float(E), None, ALU.is_ge))

            dve.wait_ge(edges_loaded, EDGE_LOADS)
            for k in range(2):
                key, hi, lo = (meta[k][:, :, j] for j in range(3))
                a, b, r = tmp[0], tmp[1], tmp[2]
                link(nc.vector.tensor_copy(a, index[k][:, :]))
                link(nc.vector.scalar_tensor_tensor(out=key, in0=pad, scalar=dumprow[:, 0:1], in1=a,
                                                    op0=ALU.mult, op1=ALU.add))
                link(nc.vector.tensor_scalar(b, a, 1.0 / C, None, ALU.mult))
                link(nc.vector.tensor_copy(tmpi, b))
                link(nc.vector.tensor_copy(b, tmpi))
                link(nc.vector.scalar_tensor_tensor(out=r, in0=b, scalar=-float(C), in1=a,
                                                    op0=ALU.mult, op1=ALU.add))
                link(nc.vector.tensor_scalar(a, r, 0.0, None, ALU.is_lt))
                link(nc.vector.tensor_tensor(b, b, a, ALU.subtract))
                link(nc.vector.scalar_tensor_tensor(out=r, in0=a, scalar=float(C), in1=r,
                                                    op0=ALU.mult, op1=ALU.add))
                link(nc.vector.tensor_scalar(a, r, float(C), None, ALU.is_ge))
                link(nc.vector.tensor_tensor(b, b, a, ALU.add))
                link(nc.vector.scalar_tensor_tensor(out=lo, in0=a, scalar=-float(C), in1=r,
                                                    op0=ALU.mult, op1=ALU.add))
                last = link(nc.vector.scalar_tensor_tensor(out=hi, in0=pad, scalar=float(2 * P), in1=b,
                                                           op0=ALU.mult, op1=ALU.add))
            dve.wait_ge(squares, 1)
            nc.vector.tensor_reduce(radial[:, :], attr.rearrange("p (t d) -> p t d", d=3), axis=AX.X,
                                    op=ALU.add).then_inc(meta_built, 1)

            def ranks(k):
                def stage(q, slot, turn):
                    g = k * PAIRS + q
                    dve.wait_ge(keys_spread, g + 1)
                    for j in range(2):
                        last = nc.vector.scalar_tensor_tensor(
                            out=junk[slot % 2][j], in0=p_key[slot % 2][:, 2 * P + j * P:2 * P + (j + 1) * P],
                            scalar=e_meta[slot][:, 3 * j:3 * j + 1], in1=tri[:, :],
                            op0=ALU.is_equal, op1=ALU.mult, accum_out=e_rank[slot][:, j:j + 1])
                    last.then_inc(ranked, 1)
                    wait(dve, counted, g)
                    for j in range(2):
                        nc.vector.tensor_scalar(hot[:, j * P:(j + 1) * P], col16[:, 0:P],
                                                e_meta[slot][:, 3 * j + 1:3 * j + 2], None, ALU.is_equal)
                        last = nc.vector.tensor_scalar(hot[:, 2 * P + j * C:2 * P + (j + 1) * C], col16[:, :],
                                                       e_meta[slot][:, 3 * j + 2:3 * j + 3], None, ALU.is_equal)
                    last.then_inc(onehot, 1)
                return stage

            def finalise(k):
                dve.wait_ge(rank_kept, (k + 1) * PAIRS)
                dve.wait_ge(hist_closed, k + 1)
                a, b = tmp[0], tmp[1]
                nc.vector.tensor_scalar(dinv[k][:, :], p_hist, 1.0, None, ALU.add).then_inc(counts_plus, 1)
                if k == 0:
                    link(nc.vector.tensor_scalar(rdeg[:, :], p_hist, 1.0, None, ALU.max))
                    link(nc.vector.reciprocal(rdeg[:, :], rdeg[:, :]))
                link(nc.vector.tensor_scalar(a, rank[:, :], 0.0, None, ALU.is_equal))
                link(nc.vector.tensor_scalar(b, meta[k][:, :, 0], dumprow[:, 0:1], None, ALU.subtract))
                link(nc.vector.tensor_tensor(b, b, a, ALU.mult))
                nc.vector.tensor_scalar(scatter[k][:, :], b, dumprow[:, 0:1], None, ALU.add).then_inc(finalised, 1)

            pipeline(dve, PAIRS, RING, [(0, ranks(0))])
            finalise(0)
            dve.wait_ge(weights_loaded, WEIGHT_LOADS)
            for m, name in enumerate(("W0", "W3")):
                dve.wait_ge(flipped, 2)
                nc.vector.tensor_copy(bd[name][:, :], p_sum[m])
            nc.vector.tensor_scalar(nalpha[:, :], alpha[:, :], -1.0, None, ALU.mult).then_inc(flip_copied, 1)
            dve.wait_ge(flip_copied, 1)
            dve.wait_ge(x_loaded, 16 * 4)

            for n in range(5):
                scale_of = {1: dinv[0], 2: dinv[1], 4: rdeg}

                def activate_z(c, slot, turn):
                    dve.wait_ge(z_sig, c + 1)
                    nc.vector.scalar_tensor_tensor(out=n_r, in0=p_nO[0], scalar=bn1c[:, 0:1], in1=n_r,
                                                   op0=ALU.add, op1=ALU.mult).then_inc(z_ready, 1)

                def finish(c, slot, turn, n=n):
                    g = (n - 1) * CHUNKS + c
                    link = linker(dve, post_step, (n - 1) * CHUNKS + c)
                    xc = x_of(c)
                    b = bias[n - 1][:, :].unsqueeze(1).to_broadcast([P, CHUNK, D])
                    dve.wait_ge(agg_out, g + 1)
                    if n == 3:
                        nc.vector.tensor_tensor(xc, xc, p_nO[1], ALU.add).then_inc(o_read, 1)
                        dve.wait_ge(o_read, g + 1)
                        link(nc.vector.tensor_tensor(grid(xc), grid(xc), b, ALU.add))
                        return
                    if n == 4:
                        wait(dve, x_new, c)
                    nc.vector.tensor_tensor(grid(n_y), grid(p_nO[slot]), spread(scale_of[n][:, cols(c)], CHUNK),
                                            ALU.mult).then_inc(o_read, 1)
                    dve.wait_ge(o_read, g + 1)
                    nc.vector.tensor_tensor(grid(n_y), grid(n_y), b, ALU.add).then_inc(biased, 1)
                    if n == 1:
                        dve.wait_ge(rectified, c + 1)
                    else:
                        dve.wait_ge(biased, g + 1 - (CHUNKS if n == 4 else 0))
                    if n == 4:
                        nc.vector.tensor_tensor(xc, xc, n_y, ALU.add).then_inc(x_new, 1)
                        return
                    link(nc.vector.tensor_tensor(xc, xc, n_y, ALU.add))
                    if n == 1:
                        nc.vector.scalar_tensor_tensor(out=xc, in0=n_r, scalar=nalpha[:, 0:1], in1=xc,
                                                       op0=ALU.mult, op1=ALU.add).then_inc(x_new1, 1)
                        dve.wait_ge(x_new1, c + 1)

                def normalise(c, slot, turn, n=n):
                    g = n * CHUNKS + c
                    xc = x_of(c)
                    if n:
                        dve.sem_inc(wait_over_v, 1)
                    link = linker(dve, ln_step, g * 3)
                    link(nc.vector.tensor_reduce(n_m, grid(xc), axis=AX.X, op=ALU.add))
                    link(nc.vector.tensor_scalar(n_m, n_m, 1.0 / D, None, ALU.mult))
                    nc.vector.tensor_tensor(grid(n_q), grid(xc), spread(n_m, CHUNK),
                                            ALU.subtract).then_inc(centred, 1)
                    dve.wait_ge(squared, g + 1)
                    dve.sem_inc(wait_over_v, 1)
                    link(nc.vector.tensor_reduce(n_v, grid(n_s), axis=AX.X, op=ALU.add))
                    nc.vector.tensor_scalar(n_v, n_v, 1.0 / D, EPS, ALU.mult, ALU.add).then_inc(var_ready, 1)
                    dve.wait_ge(rstd_ready, g + 1)
                    if n < 2:
                        nc.vector.tensor_tensor(n_v, n_v, dinv[n][:, cols(c)], ALU.mult).then_inc(scaled, 1)
                        dve.wait_ge(scaled, g + 1)
                    wait(dve, stored[slot], stores_before[n] + 16 * len(targets[n]) * turn)
                    nc.vector.scalar_tensor_tensor(out=grid(n_h[slot]), in0=grid(n_q), scalar=0.0,
                                                   in1=spread(n_v, CHUNK), op0=ALU.max,
                                                   op1=ALU.mult).then_inc(h_ready, 1)

                if n < 2:
                    dve.wait_ge(setup_pow, n + 1)
                stages = []
                if n == 3:
                    stages.append((0, activate_z))
                if n:
                    stages.append((0, finish))
                if n < 4:
                    stages.append((0, normalise))
                pipeline(dve, CHUNKS, NRING, stages)
                if n == 4:
                    break

                l = n

                def equality(q, slot, turn, l=l):
                    dve.wait_ge(key_spread, l * PAIRS + q + 1)
                    if l == L0:
                        dve.wait_ge(keys_spread, PAIRS + q + 1)
                    for j in range(2):
                        last = nc.vector.tensor_scalar(e_eq[slot][:, j * P:(j + 1) * P],
                                                       p_key[slot % 2][:, j * P:(j + 1) * P],
                                                       e_flt[slot][:, j:j + 1], None, ALU.is_equal)
                    last.then_inc(equal, 1)

                def radial_part(q, slot, turn):
                    dve.wait_ge(rows_ready, L2 * PAIRS + q + 1)
                    nc.vector.tensor_tensor(grid(e_X[slot]), wrad[:, :].unsqueeze(1).to_broadcast([P, 2, D]),
                                            spread(e_flt[slot][:, 2:4], 2), ALU.mult).then_inc(radial_term, 1)

                def silu1(q, slot, turn):
                    dve.wait_ge(sig1, q + 1)
                    wait(dve, mlp2, last_use(q, slot))
                    nc.vector.scalar_tensor_tensor(out=e_h1[slot % 2], in0=p_mlp[0], scalar=be1c[:, 0:1],
                                                   in1=e_sig1[slot % 2], op0=ALU.add,
                                                   op1=ALU.mult).then_inc(act1, 1)

                def silu2(q, slot, turn):
                    dve.wait_ge(sig2, q + 1)
                    wait(dve, natural, last_use(q, slot))
                    nc.vector.scalar_tensor_tensor(out=e_h2[slot % 2], in0=p_mlp[1], scalar=be2c[:, 0:1],
                                                   in1=e_sig2[slot % 2], op0=ALU.add,
                                                   op1=ALU.mult).then_inc(act2, 1)

                def weigh(q, slot, turn):
                    dve.wait_ge(att_ready, q + 1)
                    nc.vector.tensor_tensor(grid(e_raw[slot]), grid(p_nat[:, 0:P]), spread(e_att[slot], 2),
                                            ALU.mult).then_inc(weighted, 1)

                if l == L2:
                    pipeline(dve, PAIRS, RING, [(0, equality), (0, radial_part), (1, silu2), (0, silu1),
                                                (1, weigh)])
                elif l == L0:
                    pipeline(dve, PAIRS, RING, [(0, equality), (0, ranks(1))])
                    finalise(1)
                else:
                    pipeline(dve, PAIRS, RING, [(0, equality)])

        @block.tensor
        def _(pe):
            def open_counts(k):
                if k:
                    pe.wait_ge(finalised, k)
                nc.tensor.matmul(p_hist, zero[:, 0:P], zero[:, 0:C], start=True, stop=False)

            def close_counts():
                nc.tensor.matmul(p_hist, zero[:, 0:P], zero[:, 0:C], start=False,
                                 stop=True).then_inc(hist_closed, 1)

            def spread_keys(k):
                def stage(q, slot, turn):
                    g = k * PAIRS + q
                    pe.wait_ge(meta_ready, g + 1)
                    wait(pe, ranked, k * PAIRS + last_use(q, slot))
                    for j in range(2):
                        last = nc.tensor.matmul(p_key[slot % 2][:, 2 * P + j * P:2 * P + (j + 1) * P],
                                                e_meta[slot][:, 3 * j:3 * j + 1].to_broadcast([P, P]), ident,
                                                start=True, stop=True)
                    last.then_inc(keys_spread, 1)
                return stage

            def count(k):
                def stage(q, slot, turn):
                    pe.wait_ge(onehot, k * PAIRS + q + 1)
                    for j in range(2):
                        last = nc.tensor.matmul(p_hist, hot[:, j * P:(j + 1) * P],
                                                hot[:, 2 * P + j * C:2 * P + (j + 1) * C],
                                                start=False, stop=False)
                    last.then_inc(counted, 1)
                return stage

            pe.wait_ge(zero_ready, 1)
            pe.wait_ge(meta_built, 1)
            open_counts(0)
            pipeline(pe, PAIRS, RING, [(0, spread_keys(0)), (1, count(0))])
            close_counts()
            pe.wait_ge(weights_loaded, WEIGHT_LOADS)
            for m, name in enumerate(("W0", "W3")):
                nc.tensor.transpose(p_sum[m], bd[name][:, :], ident).then_inc(flipped, 1)
            pe.wait_ge(flip_copied, 1)

            for n in range(5):
                def turn_agg(c, slot, turn, n=n):
                    g = (n - 1) * CHUNKS + c
                    pe.wait_ge(loaded[slot], loads_before[n] + 16 * len(sources[n]) * (turn + 1))
                    wait(pe, agg_T_kept, g if n == 3 else g - 1)
                    dest = p_nT[0 if n == 3 else slot]
                    for j in range(CHUNK // 2):
                        for k in range(2):
                            last = nc.tensor.matmul(pair(dest, j), pair(n_a[k][slot], j), ident,
                                                    start=(k == 0), stop=(k == 1))
                    if n == 3:
                        for j in range(CHUNK // 2):
                            last = nc.tensor.transpose(pair(p_nT[1], j), pair(n_b, j), ident)
                    last.then_inc(agg_T, 1)

                def product(c, slot, turn, n=n):
                    g = (n - 1) * CHUNKS + c
                    pe.wait_ge(agg_T_kept, g + 1)
                    wait(pe, o_read, g - 1)
                    for j in range(CHUNK // 2):
                        last = nc.tensor.matmul(pair(p_nO[slot], j), pair(n_T, j),
                                                bd[{1: "W0", 2: "W1", 4: "W3"}[n]][:, :], start=True, stop=True)
                    last.then_inc(agg_out, 1)

                def node_mlp(c, slot, turn):
                    g = (3 - 1) * CHUNKS + c
                    pe.wait_ge(agg_T_kept, g + 1)
                    wait(pe, z_ready, c)
                    for lo, hi in ((0, 512), (512, CW)):
                        nc.tensor.matmul(p_nO[0][:, lo:hi], bd["Wn1h"][:, :], n_y[:, lo:hi], start=True, stop=False)
                        last = nc.tensor.matmul(p_nO[0][:, lo:hi], bd["Wn1a"][:, :], n_T[:, lo:hi],
                                                start=False, stop=True)
                    last.then_inc(z_out, 1)
                    pe.wait_ge(z_ready, c + 1)
                    wait(pe, o_read, g)
                    for j in range(CHUNK // 2):
                        last = nc.tensor.matmul(pair(p_nO[1], j), pair(n_r, j), bd["Wn2"][:, :],
                                                start=True, stop=True)
                    last.then_inc(agg_out, 1)

                if n:
                    pipeline(pe, CHUNKS, NRING, [(0, turn_agg), (1, node_mlp if n == 3 else product)])
                if n == 4:
                    break
                l = n

                def spread_key(q, slot, turn, l=l):
                    pe.wait_ge(rows_ready, l * PAIRS + q + 1)
                    if l == L0:
                        pe.wait_ge(ranked, PAIRS + last_use(q, slot))
                    wait(pe, equal, l * PAIRS + last_use(q, slot))
                    for j in range(2):
                        last = nc.tensor.matmul(p_key[slot % 2][:, j * P:(j + 1) * P],
                                                e_flt[slot][:, j:j + 1].to_broadcast([P, P]), ident,
                                                start=True, stop=True)
                    last.then_inc(key_spread, 1)

                def add_up(q, slot, turn, l=l):
                    rows_ = e_raw[slot] if l == L2 else e_row[0][slot]
                    if l == L2:
                        pe.wait_ge(weighted, q + 1)
                    else:
                        pe.wait_ge(gathered[slot], gathers_before[l] + 16 * 2 * tables_in[l] * (turn + 1))
                    pe.wait_ge(equal, l * PAIRS + q + 1)
                    wait(pe, msg_ready, l * PAIRS + last_use(q, slot))
                    for j in range(2):
                        last = nc.tensor.matmul(p_sum[slot % 2][:, j * D:(j + 1) * D],
                                                e_eq[slot][:, j * P:(j + 1) * P],
                                                rows_[:, j * D:(j + 1) * D], start=True, stop=True)
                    last.then_inc(summed, 1)

                def turn_rows(q, slot, turn):
                    pe.wait_ge(gathered[slot], gathers_before[L2] + 16 * 2 * tables_in[L2] * (turn + 1))
                    wait(pe, rows_T, q)
                    for k in range(2):
                        last = nc.tensor.transpose(p_T[:, k * P:(k + 1) * P], e_row[k][slot], ident)
                    last.then_inc(flipped_rows, 1)

                def edge_mlp1(q, slot, turn):
                    pe.wait_ge(rows_T, q + 1)
                    pe.wait_ge(radial_term, q + 1)
                    wait(pe, act1, q)
                    nc.tensor.matmul(p_mlp[0], bd["We1s"][:, :], e_T[slot % 2][:, 0:P], start=True, stop=False)
                    nc.tensor.matmul(p_mlp[0], bd["We1d"][:, :], e_T[slot % 2][:, P:2 * P], start=False, stop=False)
                    nc.tensor.matmul(p_mlp[0], e_X[slot], ident, start=False, stop=True).then_inc(mlp1, 1)

                def edge_mlp2(q, slot, turn):
                    pe.wait_ge(act1, q + 1)
                    wait(pe, act2, q)
                    nc.tensor.matmul(p_mlp[1], bd["We2"][:, :], e_h1[slot % 2], start=True, stop=True).then_inc(mlp2, 1)

                def turn_back(q, slot, turn):
                    pe.wait_ge(act2, q + 1)
                    wait(pe, weighted, q)
                    nc.tensor.matmul(p_nat, e_h2[slot % 2], ext[:, :], start=True, stop=True).then_inc(natural, 1)

                if l == L2:
                    pipeline(pe, PAIRS, RING, [(0, spread_key), (0, turn_rows), (1, edge_mlp2), (0, edge_mlp1),
                                               (1, turn_back), (1, add_up)])
                elif l == L0:
                    open_counts(1)
                    pipeline(pe, PAIRS, RING, [(0, spread_key), (0, spread_keys(1)), (1, count(1)), (0, add_up)])
                    close_counts()
                else:
                    pipeline(pe, PAIRS, RING, [(0, spread_key), (0, add_up)])


_INS = ['x', 'src', 'dst', 'edge_attr_3', 'L0_gnn_W', 'L0_gnn_b', 'L0_gnn_prelu_a', 'L1_gnn_weight', 'L1_gnn_bias',
        'L2_gnn_We1', 'L2_gnn_be1', 'L2_gnn_We2', 'L2_gnn_be2', 'L2_gnn_Wa', 'L2_gnn_ba', 'L2_gnn_Wn1',
        'L2_gnn_bn1', 'L2_gnn_Wn2', 'L2_gnn_bn2', 'L3_gnn_W', 'L3_gnn_b']


def kernel(**inputs):
    import numpy as _np
    import concourse.bacc as _bacc
    from concourse import mybir as _mybir
    from concourse.bass_utils import run_bass_kernel_spmd as _run

    nc = _bacc.Bacc("TRN2", target_bir_lowering=False, num_devices=1)
    arrays, args = {}, []
    for name in _INS:
        a = _np.ascontiguousarray(inputs[name])
        arrays[f"in_{name}"] = a
        args.append(nc.dram_tensor(f"in_{name}", a.shape, _mybir.dt.from_np(a.dtype), kind="ExternalInput").ap())
    out = nc.dram_tensor("out_x", (N, D), F32, kind="ExternalOutput").ap()
    gnn_kernel(nc, *args, out)
    r = _run(nc, [arrays], core_ids=[0])
    return r.results[0]["out_x"]
```

```python
from contextlib import ExitStack

import concourse.bass as bass
from concourse import mybir

F32 = mybir.dt.float32
F16 = mybir.dt.float16
I32 = mybir.dt.int32
ALU = mybir.AluOpType
ACT = mybir.ActivationFunctionType
AX = mybir.AxisListType

P = 128
N = 50000
E = 50000
D = 64
C = 392
FULL = N // C
REST = N - FULL * C
ROWS = P * C
DUMP = ROWS
EPS = 1e-5

PAIRS = C // 2
RING = 7
CHUNK = 14
CHUNKS = C // CHUNK
CW = CHUNK * D
NRING = 4
ZW = CW // 2
W2 = 2 * D

L0, L1, L2, L3 = range(4)


def wait(eng, sem, value):
    if not (isinstance(value, int) and value <= 0):
        eng.wait_ge(sem, value)


def pipeline(eng, steps, ring, stages):
    most = max(lag for lag, _ in stages)
    peeled = max(1, -(-most // ring))
    for s in range(peeled * ring):
        for lag, stage in stages:
            if s >= lag:
                stage(s - lag, (s - lag) % ring, (s - lag) // ring)
    with eng.Fori(peeled, steps // ring) as i:
        for s in range(ring):
            for lag, stage in stages:
                stage(i * ring + (s - lag), (s - lag) % ring, i + (s - lag) // ring)
    for s in range(most):
        for lag, stage in stages:
            if s < lag:
                stage(steps + s - lag, (s - lag) % ring, steps // ring + (s - lag) // ring)


def linker(eng, sem, before):
    count = [before]

    def link(ins):
        count[0] = count[0] + 1
        ins.then_inc(sem, 1)
        eng.wait_ge(sem, count[0])
    return link


def gnn_kernel(nc, x, src, dst, edge_attr, W0, b0, prelu_a, W1, b1, We1, be1, We2, be2, Wa, ba,
               Wn1, bn1, Wn2, bn2, W3, b3, out):
    table = [nc.dram_tensor(f"table{l}", [ROWS, D], F32, kind="Internal").ap() for l in range(4)]
    acc = [[nc.dram_tensor(f"acc{l}_{k}", [ROWS + P, D], F32, kind="Internal").ap() for k in range(2)]
           for l in range(4)]

    def by_partition(t):
        return t[0:ROWS, :].rearrange("(p t) d -> p (t d)", p=P)

    with ExitStack() as ctx:
        def sb(name, shape, dt=F32):
            return ctx.enter_context(nc.sbuf_tensor(name, shape, dt))

        def sem(name):
            return ctx.enter_context(nc.semaphore(name))

        xr = sb("x_resident", [P, C * D])
        index = [sb("dst_index", [P, C], I32), sb("src_index", [P, C], I32)]
        meta = [sb(f"meta{k}", [P, C, 4]) for k in range(2)]
        target = sb("target", [P, C], I32)
        dinv = [sb(f"dinv{k}", [P, C]) for k in range(2)]
        rdeg = sb("rdeg", [P, C])
        radial = sb("radial", [P, C])
        colf = sb("colf", [P, P])
        col16 = sb("col16", [P, C], F16)
        pcol = sb("pcol", [P, 1])
        dumprow = sb("dumprow", [P, 1])
        tri = sb("tri", [P, P])
        zero = sb("zero", [P, ZW])
        expo = sb("exponent", [P, 1])
        ext = sb("ident_wa", [P, P + 2])
        ident = ext[:, 0:P]
        mats = ("W0", "W1", "W3", "We1s", "We1d", "We2", "Wn1h", "Wn1a", "Wn2")
        bd = {n: sb(f"bd_{n}", [P, P]) for n in mats}
        wrad = sb("w_radial", [P, D])
        bias = [sb(f"bias{l}", [P, D]) for l in range(4)]
        be1c, be2c, bn1c, bac, alpha, nalpha = (sb(n, [P, 1]) for n in
                                                ("be1c", "be2c", "bn1c", "bac", "alpha", "nalpha"))

        ARENA = 18 * CW + 8 * CHUNK
        arena = sb("arena", [P, ARENA])
        used = [0]

        def part(n):
            used[0] += n
            assert used[0] <= ARENA, used[0]
            return arena[:, used[0] - n:used[0]]

        e_int = [part(4).bitcast(I32) for _ in range(RING)]
        e_sct = [part(2).bitcast(I32) for _ in range(RING)]
        e_flt = [part(8) for _ in range(RING)]
        e_meta = [part(8) for _ in range(RING)]
        e_rank = [part(2) for _ in range(RING)]
        e_att = [part(2) for _ in range(RING)]
        e_row = [[part(W2) for _ in range(RING)] for _ in range(2)]
        e_msg = [part(W2) for _ in range(RING)]
        e_eq = [part(2 * P) for _ in range(RING)]
        e_raw = [part(W2) for _ in range(RING)]
        e_T = [part(2 * P) for _ in range(2)]
        e_X = [part(W2) for _ in range(RING)]
        e_sig1 = [part(P) for _ in range(2)]
        e_sig2 = [part(P) for _ in range(2)]
        e_h1 = [part(P) for _ in range(2)]
        e_h2 = [part(P) for _ in range(2)]
        hot = [part(P + C).bitcast(F16) for _ in range(2)]
        junk = [[part(P) for _ in range(2)] for _ in range(2)]
        edge_used = used[0]
        attr = part(3 * C)
        tmp = [part(C) for _ in range(4)]
        tmpi = part(C).bitcast(I32)
        used[0] = 0
        n_a = [[part(CW) for _ in range(2)] for _ in range(2)]
        n_b = part(CW)
        n_T, n_y, n_r, n_h = ([part(CW) for _ in range(2)] for _ in range(4))
        n_q = [part(CW) for _ in range(NRING)]
        n_s = part(CW)
        n_m, n_v = ([part(CHUNK) for _ in range(NRING)] for _ in range(2))

        psum = ctx.enter_context(nc.psum_tensor("psum", [P, 8, 512], F32))
        p_hist = psum[:, 0, 0:C]
        p_key = [psum[:, 1 + k, :] for k in range(2)]
        p_sum = [psum[:, 3 + k, 0:W2] for k in range(2)]
        p_T = psum[:, 5, 0:2 * P]
        p_mlp = [psum[:, 6, 0:P], psum[:, 7, 0:P]]
        p_nat = psum[:, 0, 0:P + 2]
        flat = psum[:, :, :].rearrange("p b c -> p (b c)")
        p_nT = [flat[:, 2048 * 0 + 1024 * k:1024 * k + CW] for k in range(2)]
        p_nO = [flat[:, 2048 + 1024 * k:2048 + 1024 * k + CW] for k in range(2)]

        x_loaded, edges_loaded, weights_loaded = sem("x_loaded"), sem("edges_loaded"), sem("weights_loaded")
        pad_clear, iota_done, setup_step, setup_pow = (sem(n) for n in
                                                       ("pad_clear", "iota_done", "setup_step", "setup_pow"))
        zero_ready, zeroed, zeroed_later = sem("zero_ready"), sem("zeroed"), sem("zeroed_later")
        flipped, flip_copied = sem("flipped"), sem("flip_copied")
        squares = sem("attr_squares")
        meta_ready, onehot, counted = sem("meta_ready"), sem("onehot"), sem("counted")
        ranked, distance, target_made, target_kept = (sem(n) for n in
                                                      ("ranked", "distance", "target_made", "target_kept"))
        rows_ready = sem("rows_ready")
        gathered = [sem(f"gathered{s}") for s in range(RING)]
        key_spread, equal, summed, msg_ready = (sem(n) for n in ("key_spread", "equal", "summed", "msg_ready"))
        added = [sem(f"added{k}") for k in range(2)]
        flipped_rows, rows_T, radial_term = sem("flipped_rows"), sem("rows_T"), sem("radial_term")
        mlp1, sig1, act1, mlp2, sig2, act2 = (sem(n) for n in ("mlp1", "sig1", "act1", "mlp2", "sig2", "act2"))
        natural, att_ready, weighted = sem("natural"), sem("att_ready"), sem("weighted")
        loaded = [sem(f"loaded{k}") for k in range(NRING)]
        agg_T, agg_T_kept, agg_out = sem("agg_T"), sem("agg_T_kept"), sem("agg_out")
        z_out, z_sig, z_ready = sem("z_out"), sem("z_sig"), sem("z_ready")
        o_read, biased, rectified, x_new = sem("o_read"), sem("biased"), sem("rectified"), sem("x_new")
        x_part, x_sum, var_sum, norm_step, mean_ready = (sem(n) for n in
                                                         ("x_part", "x_sum", "var_sum", "norm_step", "mean_ready"))
        centred, squared, var_ready, rstd_ready, h_ready = (sem(n) for n in
                                                            ("centred", "squared", "var_ready", "rstd_ready", "h_ready"))
        stored = [sem(f"stored{k}") for k in range(NRING)]
        out_stored = sem("out_stored")

        sources = [[], [acc[0][0], acc[0][1]], [acc[1][0], acc[1][1]], [acc[2][0], acc[2][1], table[2]],
                   [acc[3][0], acc[3][1]]]
        targets = [[table[0], acc[0][0]], [table[1], acc[1][0]], [table[2]], [table[3]]]
        HALF = CHUNKS // NRING
        loads_before = [16 * HALF * sum(len(s) for s in sources[:n]) for n in range(6)]
        stores_before = [16 * HALF * sum(len(t) for t in targets[:n]) for n in range(5)]

        counts_plus, hist_closed = sem("counts_plus"), sem("hist_closed")
        wait_over, wait_over_v = sem("wait_over"), sem("wait_over_v")
        meta_built, weights_clear = sem("meta_built"), sem("weights_clear")
        parts = ((0, 96), (96, 112), (112, FULL))

        def filled(a, w):
            return a[0:FULL * C, :].rearrange("(p t) d -> p (t d)", t=C)

        def rest(a):
            return a[FULL * C:N, :].rearrange("(p t) d -> p (t d)", p=1)

        def bias_of(n):
            return bias[n - 1][:, :].unsqueeze(1).to_broadcast([P, CHUNK, D])

        def pair(t, j):
            return t[:, j * W2:(j + 1) * W2]

        def cols(c):
            return bass.ds(c * CHUNK, CHUNK)

        def spread(t, n):
            return t.unsqueeze(2).to_broadcast([P, n, D])

        def grid(t, n=CHUNK):
            return t.rearrange("p (t d) -> p t d", d=D) if len(t.shape) == 2 else t

        def x_of(c):
            return xr[:, bass.ds(c * CW, CW)]

        def last_use(q, slot):
            return q if slot == 0 else q - 1

        def key_of(l):
            return 1 if l == L2 else 0

        tables_in = [1, 1, 2, 1]
        gathers_before = [16 * 2 * (PAIRS // RING) * sum(tables_in[:l]) for l in range(4)]
        Z_FIRST = C * D // ZW
        ZERO0 = 16 * (Z_FIRST + 3)
        ZERO_LATER = 16 * 5 * (Z_FIRST + 1)
        EDGE_LOADS = 16 * 4 * 3
        WEIGHT_LOADS = 16 * (2 * len(mats) + 2 + 1 + 4 + 6 + 2)

        block = ctx.enter_context(nc.Block())

        @block.sync
        def _(sp):
            src2, dst2 = (a.rearrange("(n o) -> n o", o=1) for a in (src, dst))
            todo = [(attr, edge_attr, 3), (index[0], dst2, 1), (index[1], src2, 1)]
            for tile, a, w in todo:
                sp.dma_start(tile[0:96, :], filled(a, w)[0:96, :]).then_inc(edges_loaded, 16)
            sp.dma_start(xr[0:96, :], filled(x, D)[0:96, :]).then_inc(x_loaded, 16)
            sp.wait_ge(pad_clear, 1)
            for tile, a, w in todo:
                for lo, hi in parts[1:]:
                    sp.dma_start(tile[lo:hi, :], filled(a, w)[lo:hi, :]).then_inc(edges_loaded, 16)
                sp.dma_start(tile[FULL:P, 0:REST * w], rest(a)).then_inc(edges_loaded, 16)
            for lo, hi in parts[1:]:
                sp.dma_start(xr[lo:hi, :], filled(x, D)[lo:hi, :]).then_inc(x_loaded, 16)
            sp.dma_start(xr[FULL:P, 0:REST * D], rest(x)).then_inc(x_loaded, 16)

            def clear(a, done):
                with sp.Fori(0, Z_FIRST) as i:
                    sp.dma_start(by_partition(a)[:, bass.ds(i * ZW, ZW)], zero[:, :]).then_inc(done, 16)

            def clear_spare(a, done):
                sp.dma_start(a[DUMP:DUMP + P, :], zero[:, 0:D]).then_inc(done, 16)

            sp.wait_ge(zero_ready, 1)
            clear(acc[0][1], zeroed)
            for a in (acc[0][0], acc[0][1], acc[1][0]):
                clear_spare(a, zeroed)

            for n in range(5):
                if n == 1:
                    sp.wait_ge(rows_ready, 1)
                    for a in (acc[1][1], acc[2][0], acc[2][1], acc[3][0], acc[3][1]):
                        clear(a, zeroed_later)
                        clear_spare(a, zeroed_later)
                    sp.wait_ge(counts_plus, 2)
                    sp.wait_ge(target_kept, PAIRS)
                if n:
                    for k in range(2):
                        sp.wait_ge(added[k], 16 * PAIRS * n)

                def load(c, slot, turn, n=n):
                    wait(sp, agg_T, (n - 1) * CHUNKS + c - (0 if n == 3 else 1))
                    for buf, a in zip((n_a[0][slot % 2], n_a[1][slot % 2], n_b), sources[n]):
                        sp.dma_start(buf, by_partition(a)[:, bass.ds(c * CW, CW)]).then_inc(loaded[slot], 16)

                if n:
                    pipeline(sp, CHUNKS, NRING, [(0, load)])
            sp.wait_ge(x_new, 4 * CHUNKS)
            sp.dma_start(rest(out), xr[FULL:P, 0:REST * D]).then_inc(out_stored, 16)
            sp.wait_ge(out_stored, 16 * (2 * CHUNKS + 1))

        @block.gpsimd
        def _(pool):
            nc.gpsimd.iota(tmpi, [[1, C]], base=0, channel_multiplier=0).then_inc(iota_done, 1)
            pool.wait_ge(setup_step, 1)
            nc.gpsimd.iota(tmpi, [[1, C]], base=0, channel_multiplier=C).then_inc(iota_done, 1)
            nc.gpsimd.iota(e_int[0][:, 0:1], [[0, 1]], base=0, channel_multiplier=1)
            nc.gpsimd.iota(e_int[0][:, 1:2], [[0, 1]], base=DUMP, channel_multiplier=1)
            nc.gpsimd.memset(expo[:, :], -0.5).then_inc(iota_done, 1)

            def power(t, k):
                pool.wait_ge(counts_plus, k + 1)
                nc.gpsimd.tensor_tensor(t[:, :], t[:, :], expo[:, 0:1].to_broadcast([P, C]),
                                        ALU.pow).then_inc(setup_pow, 1)

            power(dinv[0], 0)
            for n in range(5):
                def add_bias(c, slot, turn, n=n):
                    pool.wait_ge(o_read, (n - 1) * CHUNKS + c + 1)
                    nc.gpsimd.tensor_tensor(grid(n_y[slot % 2]), grid(n_y[slot % 2]), bias_of(n),
                                            ALU.add).then_inc(biased, 1)

                def centre(c, slot, turn, n=n):
                    pool.wait_ge(mean_ready, n * CHUNKS + c + 1)
                    nc.gpsimd.tensor_tensor(grid(n_q[slot]), grid(x_of(c)), spread(n_m[slot], CHUNK),
                                            ALU.subtract).then_inc(centred, 1)

                def rstd(c, slot, turn):
                    pool.wait_ge(var_ready, 3 * CHUNKS + c + 1)
                    nc.gpsimd.tensor_tensor(n_v[slot], n_v[slot], expo[:, 0:1].to_broadcast([P, CHUNK]),
                                            ALU.pow).then_inc(rstd_ready, 1)

                pipeline(pool, CHUNKS, NRING, {0: [(0, centre)], 1: [(0, add_bias), (1, centre)],
                                               2: [(0, add_bias), (1, centre)], 3: [(0, centre), (1, rstd)],
                                               4: [(0, add_bias)]}[n])
                if n < 4:
                    l = n

                    def gather(q, slot, turn, l=l):
                        pool.wait_ge(rows_ready, l * PAIRS + q + 1)
                        pool.sem_inc(wait_over, 1)
                        for k in range(tables_in[l]):
                            for j in range(2):
                                nc.gpsimd.indirect_dma_start(
                                    out=e_row[k][slot][:, j * D:(j + 1) * D], out_offset=None, in_=table[l][:, :],
                                    in_offset=bass.IndirectOffsetOnAxis(
                                        ap=e_int[slot][:, 2 * k + j:2 * k + j + 1], axis=0),
                                ).then_inc(gathered[slot], 16)

                    def add(q, slot, turn, l=l):
                        pool.wait_ge(msg_ready, l * PAIRS + q + 1)
                        if l in (L0, L2):
                            pool.wait_ge(target_made, key_of(l) * PAIRS + q + 1)
                        for j in range(2):
                            wait(pool, added[j], 16 * (l * PAIRS + q))
                            pool.sem_inc(wait_over, 1)
                            nc.gpsimd.indirect_dma_start(
                                out=acc[l][j][:, :],
                                out_offset=bass.IndirectOffsetOnAxis(ap=e_sct[slot][:, j:j + 1], axis=0),
                                in_=e_msg[slot][:, j * D:(j + 1) * D], in_offset=None,
                                compute_op=ALU.add).then_inc(added[j], 16)

                    if l == L0:
                        pool.wait_ge(zeroed, ZERO0)
                    else:
                        pool.wait_ge(zeroed_later, ZERO_LATER)
                    pipeline(pool, PAIRS, RING, [(0, gather), (4 if l == L2 else 3, add)])
                    if l == 0:
                        power(dinv[1], 1)

        @block.scalar
        def _(act):
            def load(dst_, src_):
                act.dma_start(dst_, src_).then_inc(weights_loaded, 16)

            act.wait_ge(weights_clear, 1)
            blocks = {"W0": W0, "W1": W1, "W3": W3, "We1s": We1[0:D, :], "We1d": We1[D:2 * D, :], "We2": We2,
                      "Wn1h": Wn1[D - D:D, :], "Wn1a": Wn1[D:2 * D, :], "Wn2": Wn2}
            for name in mats:
                for h in range(2):
                    load(bd[name][h * D:(h + 1) * D, h * D:(h + 1) * D], blocks[name])
            for h in range(2):
                load(ext[h * D:(h + 1) * D, P + h:P + h + 1], Wa)
            load(wrad[:, :], We1[2 * D:2 * D + 1, :].to_broadcast([P, D]))
            for l, b in enumerate((b0, b1, bn2, b3)):
                load(bias[l][:, :], b.rearrange("(o d) -> o d", o=1).to_broadcast([P, D]))
            for t, b in ((be1c, be1), (be2c, be2), (bn1c, bn1)):
                for h in range(2):
                    load(t[h * D:(h + 1) * D, :], b.rearrange("(d o) -> d o", o=1))
            for t, b in ((bac, ba), (alpha, prelu_a)):
                load(t[:, :], b.rearrange("(o d) -> o d", o=1).to_broadcast([P, 1]))
            act.wait_ge(edges_loaded, EDGE_LOADS)
            nc.scalar.activation(attr, attr, ACT.Square).then_inc(squares, 1)

            def index_load(k):
                def stage(q, slot, turn):
                    wait(act, counted, k * PAIRS + q - RING + 1)
                    nc.scalar.copy(e_meta[slot].rearrange("p (a b) -> p a b", b=4),
                                   meta[k][:, bass.ds(2 * q, 2), :]).then_inc(meta_ready, 1)
                return stage

            act.wait_ge(meta_built, 1)
            pipeline(act, PAIRS, RING, [(0, index_load(0))])

            for n in range(5):
                def keep_T(c, slot, turn, n=n):
                    g = (n - 1) * CHUNKS + c
                    act.wait_ge(agg_T, g + 1)
                    wait(act, agg_out, g - 1)
                    last = nc.scalar.copy(n_T[slot % 2], p_nT[0 if n == 3 else slot % 2])
                    if n == 3:
                        last = nc.scalar.copy(n_y[slot % 2], p_nT[1])
                    last.then_inc(agg_T_kept, 1)

                def rectify(c, slot, turn):
                    act.wait_ge(biased, c + 1)
                    nc.scalar.activation(n_r[slot % 2], n_y[slot % 2], ACT.Relu, scale=-1.0)
                    nc.scalar.activation(n_y[slot % 2], n_y[slot % 2], ACT.Relu).then_inc(rectified, 1)

                def z_sigmoid(c, slot, turn):
                    act.wait_ge(z_out, c + 1)
                    nc.scalar.activation(n_r[slot % 2], p_nO[0], ACT.Sigmoid, bias=bn1c[:, 0:1]).then_inc(z_sig, 1)

                def square(c, slot, turn, n=n):
                    act.wait_ge(centred, n * CHUNKS + c + 1)
                    wait(act, var_ready, n * CHUNKS + c)
                    nc.scalar.activation(n_s, n_q[slot], ACT.Square).then_inc(squared, 1)

                def root(c, slot, turn, n=n):
                    act.wait_ge(var_ready, n * CHUNKS + c + 1)
                    nc.scalar.activation(n_v[slot], n_v[slot], ACT.Sqrt).then_inc(rstd_ready, 1)

                def store(c, slot, turn, n=n):
                    act.wait_ge(h_ready, n * CHUNKS + c + 1)
                    for a in targets[n]:
                        act.dma_start(by_partition(a)[:, bass.ds(c * CW, CW)],
                                      n_h[slot % 2]).then_inc(stored[slot], 16)

                def store_out(c, slot, turn):
                    act.wait_ge(x_new, 3 * CHUNKS + c + 1)
                    for lo, hi in ((0, 112), (112, FULL)):
                        act.dma_start(filled(out, D)[lo:hi, bass.ds(c * CW, CW)],
                                      xr[lo:hi, bass.ds(c * CW, CW)]).then_inc(out_stored, 16)

                stages = []
                if n:
                    stages.append((0, keep_T))
                if n == 1:
                    stages.append((1, rectify))
                if n == 3:
                    stages.append((1, z_sigmoid))
                if n < 3:
                    stages.append((3, root))
                if n < 4:
                    stages.append((2, square))
                    stages.append((5, store))
                else:
                    stages.append((3, store_out))
                pipeline(act, CHUNKS, NRING, stages)
                if n == 4:
                    break

                l, k = n, key_of(n)
                if l == L1:
                    act.wait_ge(target_kept, PAIRS)
                for s in range(NRING):
                    act.wait_ge(stored[s], stores_before[l + 1])

                def rows(q, slot, turn, l=l, k=k):
                    for j in range(2):
                        wait(act, added[j], 16 * (l * PAIRS + q - RING + 1))
                    two = bass.ds(2 * q, 2)
                    nc.scalar.copy(e_int[slot][:, 0:2], index[1][:, two])
                    if l == L2:
                        nc.scalar.copy(e_int[slot][:, 2:4], index[0][:, two])
                        nc.scalar.copy(e_flt[slot][:, 4:6], radial[:, two])
                    if l in (L1, L3):
                        nc.scalar.copy(e_sct[slot], target[:, two])
                    nc.scalar.copy(e_flt[slot][:, 0:4].rearrange("p (a b) -> p a b", b=2),
                                   meta[k][:, two, 0:2]).then_inc(rows_ready, 1)

                def keep_target(q, slot, turn):
                    act.wait_ge(target_made, q + 1)
                    nc.scalar.copy(target[:, bass.ds(2 * q, 2)], e_sct[slot]).then_inc(target_kept, 1)

                def message(q, slot, turn, l=l):
                    act.wait_ge(summed, l * PAIRS + q + 1)
                    nc.scalar.copy(e_msg[slot], p_sum[slot % 2]).then_inc(msg_ready, 1)

                def keep_rows_T(q, slot, turn):
                    act.wait_ge(flipped_rows, q + 1)
                    wait(act, mlp1, last_use(q, slot))
                    nc.scalar.copy(e_T[slot % 2], p_T).then_inc(rows_T, 1)

                def sigmoid1(q, slot, turn):
                    act.wait_ge(mlp1, q + 1)
                    wait(act, act1, last_use(q, slot))
                    nc.scalar.activation(e_sig1[slot % 2], p_mlp[0], ACT.Sigmoid,
                                         bias=be1c[:, 0:1]).then_inc(sig1, 1)

                def sigmoid2(q, slot, turn):
                    act.wait_ge(mlp2, q + 1)
                    wait(act, act2, last_use(q, slot))
                    nc.scalar.activation(e_sig2[slot % 2], p_mlp[1], ACT.Sigmoid,
                                         bias=be2c[:, 0:1]).then_inc(sig2, 1)

                def attention(q, slot, turn):
                    act.wait_ge(natural, q + 1)
                    nc.scalar.activation(e_att[slot], p_nat[:, P:P + 2], ACT.Sigmoid,
                                         bias=bac[:, 0:1]).then_inc(att_ready, 1)

                if l == L2:
                    pipeline(act, PAIRS, RING, [(0, rows), (2, keep_rows_T), (3, sigmoid2), (2, sigmoid1),
                                                (3, attention), (3, message)])
                elif l == L0:
                    pipeline(act, PAIRS, RING, [(0, rows), (0, index_load(1)), (2, keep_target), (2, message)])
                else:
                    pipeline(act, PAIRS, RING, [(0, rows), (2, message)])

        @block.vector
        def _(dve):
            nc.vector.memset(xr[96:P, REST * D:], 0.0)
            for t, w in ((attr, 3), (index[0], 1), (index[1], 1)):
                last = nc.vector.memset(t[96:P, REST * w:], 0)
            last.then_inc(pad_clear, 1)
            for name in mats:
                nc.vector.memset(bd[name][:, :], 0.0)
            nc.vector.memset(ext[:, P:P + 2], 0.0).then_inc(weights_clear, 1)
            nc.vector.memset(zero[:, :], 0.0).then_inc(zero_ready, 1)

            link = linker(dve, setup_step, 0)
            dve.wait_ge(iota_done, 1)
            link(nc.vector.tensor_copy(tmp[0], tmpi))
            nc.vector.tensor_copy(colf[:, :], tmp[0][:, 0:P])
            link(nc.vector.tensor_copy(col16[:, :], tmp[0]))
            dve.wait_ge(iota_done, 3)
            link(nc.vector.tensor_copy(pcol[:, :], e_int[0][:, 0:1]))
            link(nc.vector.tensor_copy(dumprow[:, :], e_int[0][:, 1:2]))
            nc.vector.tensor_scalar(ident, colf[:, :], pcol[:, 0:1], None, ALU.is_equal)
            nc.vector.tensor_scalar(tri[:, :], colf[:, :], pcol[:, 0:1], None, ALU.is_lt)
            pad = tmp[3]
            link(nc.vector.tensor_copy(pad, tmpi))
            link(nc.vector.tensor_scalar(pad, pad, float(E), None, ALU.is_ge))

            dve.wait_ge(edges_loaded, EDGE_LOADS)
            for k in range(2):
                key, dist, hi, lo = (meta[k][:, :, j] for j in range(4))
                a, b, r = tmp[0], tmp[1], tmp[2]
                link(nc.vector.tensor_copy(a, index[k][:, :]))
                link(nc.vector.scalar_tensor_tensor(out=key, in0=pad, scalar=dumprow[:, 0:1], in1=a,
                                                    op0=ALU.mult, op1=ALU.add))
                link(nc.vector.tensor_scalar(dist, key, dumprow[:, 0:1], None, ALU.subtract))
                link(nc.vector.tensor_scalar(b, a, 1.0 / C, None, ALU.mult))
                link(nc.vector.tensor_copy(tmpi, b))
                link(nc.vector.tensor_copy(b, tmpi))
                link(nc.vector.scalar_tensor_tensor(out=r, in0=b, scalar=-float(C), in1=a,
                                                    op0=ALU.mult, op1=ALU.add))
                link(nc.vector.tensor_scalar(a, r, 0.0, None, ALU.is_lt))
                link(nc.vector.tensor_tensor(b, b, a, ALU.subtract))
                link(nc.vector.scalar_tensor_tensor(out=r, in0=a, scalar=float(C), in1=r,
                                                    op0=ALU.mult, op1=ALU.add))
                link(nc.vector.tensor_scalar(a, r, float(C), None, ALU.is_ge))
                link(nc.vector.tensor_tensor(b, b, a, ALU.add))
                link(nc.vector.scalar_tensor_tensor(out=lo, in0=a, scalar=-float(C), in1=r,
                                                    op0=ALU.mult, op1=ALU.add))
                last = link(nc.vector.scalar_tensor_tensor(out=hi, in0=pad, scalar=float(2 * P), in1=b,
                                                           op0=ALU.mult, op1=ALU.add))
            dve.wait_ge(squares, 1)
            nc.vector.tensor_reduce(radial[:, :], attr.rearrange("p (t d) -> p t d", d=3), axis=AX.X,
                                    op=ALU.add).then_inc(meta_built, 1)

            def one_hots(k):
                def stage(q, slot, turn):
                    g = k * PAIRS + q
                    dve.wait_ge(meta_ready, g + 1)
                    wait(dve, counted, k * PAIRS + last_use(q, slot))
                    buf = hot[slot % 2]
                    for j in range(2):
                        nc.vector.tensor_scalar(buf[:, j * P:(j + 1) * P], col16[:, 0:P],
                                                e_meta[slot][:, 4 * j + 2:4 * j + 3], None, ALU.is_equal)
                        last = nc.vector.tensor_scalar(buf[:, 2 * P + j * C:2 * P + (j + 1) * C], col16[:, :],
                                                       e_meta[slot][:, 4 * j + 3:4 * j + 4], None, ALU.is_equal)
                    last.then_inc(onehot, 1)
                return stage

            def finalise(k):
                dve.wait_ge(hist_closed, k + 1)
                last = nc.vector.tensor_scalar(dinv[k][:, :], p_hist, 1.0, None, ALU.add)
                last.then_inc(counts_plus, 1)
                if k == 0:
                    link(nc.vector.tensor_scalar(rdeg[:, :], p_hist, 1.0, None, ALU.max))
                    link(nc.vector.reciprocal(rdeg[:, :], rdeg[:, :]))

            pipeline(dve, PAIRS, RING, [(0, one_hots(0))])
            finalise(0)
            dve.wait_ge(weights_loaded, WEIGHT_LOADS)
            for m, name in enumerate(("W0", "W3")):
                dve.wait_ge(flipped, 2)
                nc.vector.tensor_copy(bd[name][:, :], p_sum[m])
            nc.vector.tensor_scalar(nalpha[:, :], alpha[:, :], -1.0, None, ALU.mult).then_inc(flip_copied, 1)
            dve.wait_ge(flip_copied, 1)
            dve.wait_ge(x_loaded, 16 * 4)

            for n in range(5):
                def scale(c, slot, turn, n=n):
                    g = (n - 1) * CHUNKS + c
                    factor = {1: dinv[0], 2: dinv[1], 4: rdeg}[n]
                    dve.wait_ge(agg_out, g + 1)
                    wait(dve, x_new, g - 1)
                    nc.vector.tensor_tensor(grid(n_y[slot % 2]), grid(p_nO[slot % 2]),
                                            spread(factor[:, cols(c)], CHUNK), ALU.mult).then_inc(o_read, 1)

                def activate_z(c, slot, turn):
                    dve.wait_ge(z_sig, c + 1)
                    nc.vector.scalar_tensor_tensor(out=n_r[slot % 2], in0=p_nO[0], scalar=bn1c[:, 0:1],
                                                   in1=n_r[slot % 2], op0=ALU.add,
                                                   op1=ALU.mult).then_inc(z_ready, 1)

                def residual(c, slot, turn, n=n):
                    g = (n - 1) * CHUNKS + c
                    xc = x_of(c)
                    if n == 1:
                        dve.wait_ge(rectified, c + 1)
                        nc.vector.tensor_tensor(xc, xc, n_y[slot % 2], ALU.add).then_inc(x_part, 1)
                        dve.wait_ge(x_part, c + 1)
                        nc.vector.scalar_tensor_tensor(out=xc, in0=n_r[slot % 2], scalar=nalpha[:, 0:1], in1=xc,
                                                       op0=ALU.mult, op1=ALU.add).then_inc(x_new, 1)
                    elif n == 3:
                        dve.wait_ge(agg_out, g + 1)
                        nc.vector.tensor_tensor(xc, xc, p_nO[1], ALU.add).then_inc(o_read, 1)
                        dve.wait_ge(o_read, g + 1)
                        nc.vector.tensor_tensor(grid(xc), grid(xc), bias_of(n), ALU.add).then_inc(x_new, 1)
                    elif n:
                        dve.wait_ge(biased, g + 1 - (CHUNKS if n == 4 else 0))
                        nc.vector.tensor_tensor(xc, xc, n_y[slot % 2], ALU.add).then_inc(x_new, 1)
                    if n == 4:
                        return
                    if n:
                        dve.wait_ge(x_new, g + 1)
                        dve.sem_inc(wait_over_v, 1)
                    nc.vector.tensor_reduce(n_m[slot], grid(xc), axis=AX.X, op=ALU.add).then_inc(x_sum, 1)
                    dve.wait_ge(x_sum, n * CHUNKS + c + 1)
                    nc.vector.tensor_scalar(n_m[slot], n_m[slot], 1.0 / D, None, ALU.mult).then_inc(mean_ready, 1)

                def variance(c, slot, turn, n=n):
                    g = n * CHUNKS + c
                    dve.wait_ge(squared, g + 1)
                    dve.sem_inc(wait_over_v, 1)
                    nc.vector.tensor_reduce(n_v[slot], grid(n_s), axis=AX.X, op=ALU.add).then_inc(var_sum, 1)
                    dve.wait_ge(var_sum, g + 1)
                    nc.vector.tensor_scalar(n_v[slot], n_v[slot], 1.0 / D, EPS, ALU.mult,
                                            ALU.add).then_inc(var_ready, 1)

                def normalise(c, slot, turn, n=n):
                    g = n * CHUNKS + c
                    link = linker(dve, norm_step, {0: c * 2, 1: c * 2 + 2 * CHUNKS, 2: c + 4 * CHUNKS, 3: 0}[n])
                    dve.wait_ge(rstd_ready, g + 1)
                    if n < 3:
                        link(nc.vector.reciprocal(n_v[slot], n_v[slot]))
                    if n < 2:
                        link(nc.vector.tensor_tensor(n_v[slot], n_v[slot], dinv[n][:, cols(c)], ALU.mult))
                    before = stores_before[n] + 16 * len(targets[n]) * (turn + 1 if slot >= 2 else turn)
                    wait(dve, stored[(slot + 2) % NRING], before)
                    nc.vector.scalar_tensor_tensor(out=grid(n_h[slot % 2]), in0=grid(n_q[slot]), scalar=0.0,
                                                   in1=spread(n_v[slot], CHUNK), op0=ALU.max,
                                                   op1=ALU.mult).then_inc(h_ready, 1)

                if n < 2:
                    dve.wait_ge(setup_pow, n + 1)
                stages = [(0, activate_z if n == 3 else scale)] if n else []
                stages.append((1, residual))
                if n < 4:
                    stages += [(2, variance), (3, normalise)]
                pipeline(dve, CHUNKS, NRING, stages)
                if n == 4:
                    break

                l = n

                def equality(q, slot, turn, l=l):
                    dve.wait_ge(key_spread, l * PAIRS + q + 1)
                    g = key_of(l) * PAIRS + q
                    keys = [p_key[slot % 2][:, j * P:(j + 1) * P] for j in range(2)]
                    if l in (L0, L2):
                        for j in range(2):
                            last = nc.vector.scalar_tensor_tensor(
                                out=junk[slot % 2][j], in0=keys[j], scalar=e_flt[slot][:, 2 * j:2 * j + 1],
                                in1=tri[:, :], op0=ALU.is_equal, op1=ALU.mult, accum_out=e_rank[slot][:, j:j + 1])
                        last.then_inc(ranked, 1)
                    for j in range(2):
                        last = nc.vector.tensor_scalar(e_eq[slot][:, j * P:(j + 1) * P], keys[j],
                                                       e_flt[slot][:, 2 * j:2 * j + 1], None, ALU.is_equal)
                    last.then_inc(equal, 1)
                    if l in (L0, L2):
                        dve.wait_ge(ranked, g + 1)
                        nc.vector.scalar_tensor_tensor(
                            out=e_rank[slot], in0=e_rank[slot], scalar=0.0, in1=e_flt[slot][:, 1:4:2],
                            op0=ALU.is_equal, op1=ALU.mult).then_inc(distance, 1)
                        dve.wait_ge(distance, g + 1)
                        nc.vector.tensor_scalar(e_sct[slot], e_rank[slot], dumprow[:, 0:1], None,
                                                ALU.add).then_inc(target_made, 1)

                def radial_part(q, slot, turn):
                    dve.wait_ge(rows_ready, L2 * PAIRS + q + 1)
                    nc.vector.tensor_tensor(grid(e_X[slot]), wrad[:, :].unsqueeze(1).to_broadcast([P, 2, D]),
                                            spread(e_flt[slot][:, 4:6], 2), ALU.mult).then_inc(radial_term, 1)

                def silu1(q, slot, turn):
                    dve.wait_ge(sig1, q + 1)
                    wait(dve, mlp2, last_use(q, slot))
                    nc.vector.scalar_tensor_tensor(out=e_h1[slot % 2], in0=p_mlp[0], scalar=be1c[:, 0:1],
                                                   in1=e_sig1[slot % 2], op0=ALU.add,
                                                   op1=ALU.mult).then_inc(act1, 1)

                def silu2(q, slot, turn):
                    dve.wait_ge(sig2, q + 1)
                    wait(dve, natural, last_use(q, slot))
                    nc.vector.scalar_tensor_tensor(out=e_h2[slot % 2], in0=p_mlp[1], scalar=be2c[:, 0:1],
                                                   in1=e_sig2[slot % 2], op0=ALU.add,
                                                   op1=ALU.mult).then_inc(act2, 1)

                def weigh(q, slot, turn):
                    dve.wait_ge(att_ready, q + 1)
                    nc.vector.tensor_tensor(grid(e_raw[slot]), grid(p_nat[:, 0:P]), spread(e_att[slot], 2),
                                            ALU.mult).then_inc(weighted, 1)

                if l == L2:
                    pipeline(dve, PAIRS, RING, [(0, equality), (0, radial_part), (1, silu2), (0, silu1),
                                                (1, weigh)])
                elif l == L0:
                    pipeline(dve, PAIRS, RING, [(0, equality), (0, one_hots(1))])
                    finalise(1)
                else:
                    pipeline(dve, PAIRS, RING, [(0, equality)])

        @block.tensor
        def _(pe):
            def open_counts(k):
                nc.tensor.matmul(p_hist, zero[:, 0:P], zero[:, 0:C], start=True, stop=False)

            def close_counts():
                nc.tensor.matmul(p_hist, zero[:, 0:P], zero[:, 0:C], start=False,
                                 stop=True).then_inc(hist_closed, 1)

            def count(k):
                def stage(q, slot, turn):
                    pe.wait_ge(onehot, k * PAIRS + q + 1)
                    for j in range(2):
                        last = nc.tensor.matmul(p_hist, hot[slot % 2][:, j * P:(j + 1) * P],
                                                hot[slot % 2][:, 2 * P + j * C:2 * P + (j + 1) * C],
                                                start=False, stop=False)
                    last.then_inc(counted, 1)
                return stage

            pe.wait_ge(zero_ready, 1)
            pe.wait_ge(meta_built, 1)
            open_counts(0)
            pipeline(pe, PAIRS, RING, [(0, count(0))])
            close_counts()
            pe.wait_ge(weights_loaded, WEIGHT_LOADS)
            for m, name in enumerate(("W0", "W3")):
                nc.tensor.transpose(p_sum[m], bd[name][:, :], ident).then_inc(flipped, 1)
            pe.wait_ge(flip_copied, 1)

            for n in range(5):
                def turn_agg(c, slot, turn, n=n):
                    g = (n - 1) * CHUNKS + c
                    pe.wait_ge(loaded[slot], loads_before[n] + 16 * len(sources[n]) * (turn + 1))
                    wait(pe, agg_T_kept, g if n == 3 else g - 1)
                    dest = p_nT[0 if n == 3 else slot % 2]
                    for j in range(CHUNK // 2):
                        for k in range(2):
                            last = nc.tensor.matmul(pair(dest, j), pair(n_a[k][slot % 2], j), ident,
                                                    start=(k == 0), stop=(k == 1), is_transpose=True)
                    if n == 3:
                        for j in range(CHUNK // 2):
                            last = nc.tensor.transpose(pair(p_nT[1], j), pair(n_b, j), ident)
                    last.then_inc(agg_T, 1)

                def product(c, slot, turn, n=n):
                    g = (n - 1) * CHUNKS + c
                    pe.wait_ge(agg_T_kept, g + 1)
                    wait(pe, o_read, g - 1)
                    for j in range(CHUNK // 2):
                        last = nc.tensor.matmul(pair(p_nO[slot % 2], j), pair(n_T[slot % 2], j),
                                                bd[{1: "W0", 2: "W1", 4: "W3"}[n]][:, :], start=True, stop=True)
                    last.then_inc(agg_out, 1)

                def node_mlp(c, slot, turn):
                    g = (3 - 1) * CHUNKS + c
                    pe.wait_ge(agg_T_kept, g + 1)
                    wait(pe, z_ready, c)
                    for lo, hi in ((0, 512), (512, CW)):
                        nc.tensor.matmul(p_nO[0][:, lo:hi], bd["Wn1h"][:, :], n_y[slot % 2][:, lo:hi], start=True, stop=False)
                        last = nc.tensor.matmul(p_nO[0][:, lo:hi], bd["Wn1a"][:, :], n_T[slot % 2][:, lo:hi],
                                                start=False, stop=True)
                    last.then_inc(z_out, 1)
                    pe.wait_ge(z_ready, c + 1)
                    wait(pe, o_read, g)
                    for j in range(CHUNK // 2):
                        last = nc.tensor.matmul(pair(p_nO[1], j), pair(n_r[slot % 2], j), bd["Wn2"][:, :],
                                                start=True, stop=True)
                    last.then_inc(agg_out, 1)

                if n:
                    pipeline(pe, CHUNKS, NRING, [(0, turn_agg), (1, node_mlp if n == 3 else product)])
                if n == 4:
                    break
                l = n

                def spread_key(q, slot, turn, l=l):
                    pe.wait_ge(rows_ready, l * PAIRS + q + 1)
                    wait(pe, equal, l * PAIRS + last_use(q, slot))
                    for j in range(2):
                        last = nc.tensor.transpose(p_key[slot % 2][:, j * P:(j + 1) * P],
                                                   e_flt[slot][:, 2 * j:2 * j + 1].to_broadcast([P, P]), ident)
                    last.then_inc(key_spread, 1)

                def add_up(q, slot, turn, l=l):
                    rows_ = e_raw[slot] if l == L2 else e_row[0][slot]
                    if l == L2:
                        pe.wait_ge(weighted, q + 1)
                    else:
                        pe.wait_ge(gathered[slot], gathers_before[l] + 16 * 2 * tables_in[l] * (turn + 1))
                    pe.wait_ge(equal, l * PAIRS + q + 1)
                    wait(pe, msg_ready, l * PAIRS + last_use(q, slot))
                    for j in range(2):
                        last = nc.tensor.matmul(p_sum[slot % 2][:, j * D:(j + 1) * D],
                                                e_eq[slot][:, j * P:(j + 1) * P],
                                                rows_[:, j * D:(j + 1) * D], start=True, stop=True)
                    last.then_inc(summed, 1)

                def turn_rows(q, slot, turn):
                    pe.wait_ge(gathered[slot], gathers_before[L2] + 16 * 2 * tables_in[L2] * (turn + 1))
                    wait(pe, rows_T, q)
                    for k in range(2):
                        last = nc.tensor.transpose(p_T[:, k * P:(k + 1) * P], e_row[k][slot], ident)
                    last.then_inc(flipped_rows, 1)

                def edge_mlp1(q, slot, turn):
                    pe.wait_ge(rows_T, q + 1)
                    pe.wait_ge(radial_term, q + 1)
                    wait(pe, act1, q)
                    nc.tensor.matmul(p_mlp[0], bd["We1s"][:, :], e_T[slot % 2][:, 0:P], start=True, stop=False)
                    nc.tensor.matmul(p_mlp[0], bd["We1d"][:, :], e_T[slot % 2][:, P:2 * P], start=False, stop=False)
                    nc.tensor.matmul(p_mlp[0], e_X[slot], ident, start=False, stop=True).then_inc(mlp1, 1)

                def edge_mlp2(q, slot, turn):
                    pe.wait_ge(act1, q + 1)
                    wait(pe, act2, q)
                    nc.tensor.matmul(p_mlp[1], bd["We2"][:, :], e_h1[slot % 2], start=True, stop=True).then_inc(mlp2, 1)

                def turn_back(q, slot, turn):
                    pe.wait_ge(act2, q + 1)
                    wait(pe, weighted, q)
                    nc.tensor.matmul(p_nat, e_h2[slot % 2], ext[:, :], start=True, stop=True).then_inc(natural, 1)

                if l == L2:
                    pipeline(pe, PAIRS, RING, [(0, spread_key), (0, turn_rows), (1, edge_mlp2), (0, edge_mlp1),
                                               (1, turn_back), (1, add_up)])
                elif l == L0:
                    open_counts(1)
                    pipeline(pe, PAIRS, RING, [(0, spread_key), (1, count(1)), (0, add_up)])
                    close_counts()
                else:
                    pipeline(pe, PAIRS, RING, [(0, spread_key), (0, add_up)])


_INS = ['x', 'src', 'dst', 'edge_attr_3', 'L0_gnn_W', 'L0_gnn_b', 'L0_gnn_prelu_a', 'L1_gnn_weight', 'L1_gnn_bias',
        'L2_gnn_We1', 'L2_gnn_be1', 'L2_gnn_We2', 'L2_gnn_be2', 'L2_gnn_Wa', 'L2_gnn_ba', 'L2_gnn_Wn1',
        'L2_gnn_bn1', 'L2_gnn_Wn2', 'L2_gnn_bn2', 'L3_gnn_W', 'L3_gnn_b']


def kernel(**inputs):
    import numpy as _np
    import concourse.bacc as _bacc
    from concourse import mybir as _mybir
    from concourse.bass_utils import run_bass_kernel_spmd as _run

    nc = _bacc.Bacc("TRN2", target_bir_lowering=False, num_devices=1)
    arrays, args = {}, []
    for name in _INS:
        a = _np.ascontiguousarray(inputs[name])
        arrays[f"in_{name}"] = a
        args.append(nc.dram_tensor(f"in_{name}", a.shape, _mybir.dt.from_np(a.dtype), kind="ExternalInput").ap())
    out = nc.dram_tensor("out_x", (N, D), F32, kind="ExternalOutput").ap()
    gnn_kernel(nc, *args, out)
    r = _run(nc, [arrays], core_ids=[0])
    return r.results[0]["out_x"]
```

```python
from contextlib import ExitStack

import concourse.bass as bass
from concourse import mybir

F32 = mybir.dt.float32
F16 = mybir.dt.float16
BF16 = mybir.dt.bfloat16
I32 = mybir.dt.int32
ALU = mybir.AluOpType
ACT = mybir.ActivationFunctionType
AX = mybir.AxisListType

P = 128
N = 50000
E = 50000
D = 64
C = 392
NODE_TILES = N // P
NODE_REST = N - NODE_TILES * P
EDGE_TILES = E // P
EDGE_REST = E - EDGE_TILES * P
ROWS = P * C
DUMP = ROWS
EPS = 1e-5

PAIRS = C // 2
RING = 7
CHUNK = 14
CHUNKS = C // CHUNK
CW = CHUNK * D
NRING = 4
ZW = CW // 2
WIN = 4
WP = WIN * P
WD = WIN * D
GROUPS = 4
GP = C // GROUPS
D3 = 3 * D
W2 = 2 * D

SHIFT = P.bit_length() - 1

L0, L1, L2, L3 = range(4)


def wait(eng, sem, value):
    if not (isinstance(value, int) and value <= 0):
        eng.wait_ge(sem, value)


def pipeline(eng, steps, ring, stages):
    most = max(lag for lag, _ in stages)
    peeled = max(1, -(-most // ring))
    for s in range(peeled * ring):
        for lag, stage in stages:
            if s >= lag:
                stage(s - lag, (s - lag) % ring, (s - lag) // ring)
    with eng.Fori(peeled, steps // ring) as i:
        for s in range(ring):
            for lag, stage in stages:
                stage(i * ring + (s - lag), (s - lag) % ring, i + (s - lag) // ring)
    for s in range(most):
        for lag, stage in stages:
            if s < lag:
                stage(steps + s - lag, (s - lag) % ring, steps // ring + (s - lag) // ring)


def linker(eng, sem, before):
    count = [before]

    def link(ins):
        count[0] = count[0] + 1
        ins.then_inc(sem, 1)
        eng.wait_ge(sem, count[0])
    return link


def gnn_kernel(nc, x, src, dst, edge_attr, W0, b0, prelu_a, W1, b1, We1, be1, We2, be2, Wa, ba,
               Wn1, bn1, Wn2, bn2, W3, b3, out):
    xs = nc.dram_tensor("x_scratch", [P, C * D], F32, kind="Internal").ap()
    table = [nc.dram_tensor(f"table{l}", [ROWS, D if l == L2 else D3], F32 if l == L2 else BF16,
                            kind="Internal").ap() for l in range(4)]
    acc = [nc.dram_tensor(f"acc{k}", [ROWS + P, D], F32, kind="Internal").ap() for k in range(2)]
    acc_s = nc.dram_tensor("acc_stragglers", [ROWS + P, D], F32, kind="Internal").ap()

    def by_partition(t):
        return t[0:ROWS, :].rearrange("(p t) d -> p (t d)", p=P)

    with ExitStack() as ctx:
        def sb(name, shape, dt=F32):
            return ctx.enter_context(nc.sbuf_tensor(name, shape, dt))

        def sem(name):
            return ctx.enter_context(nc.semaphore(name))

        agg = sb("aggregate", [P, C * D])
        index = [sb("dst_row", [P, C], I32), sb("src_row", [P, C], I32)]
        meta = [sb(f"meta{k}", [P, C, 4]) for k in range(2)]
        krel = sb("window_key", [P, C])
        window = sb("window_start", [P, C], I32)
        missed = sb("missed", [P, C])
        flag = sb("any_missed", [1, 1], I32)
        dinv = [sb(f"dinv{k}", [P, C]) for k in range(2)]
        rdeg = sb("rdeg", [P, C])
        radial = sb("radial", [P, C])
        colf = sb("colf", [P, P])
        col16 = sb("col16", [P, WP], F16)
        pcol = sb("pcol", [P, 1])
        dumprow = sb("dumprow", [P, 1])
        tri = sb("tri", [P, P])
        zero = sb("zero", [P, ZW])
        expo = sb("exponent", [P, 1])
        ones = sb("ones", [1, P])
        ext = sb("ident_wa", [P, P + 2])
        ident = ext[:, 0:P]
        mats = ("W0", "W1", "W3", "We1s", "We1d", "We2", "Wn1h", "Wn1a", "Wn2")
        bd = {n: sb(f"bd_{n}", [P, P]) for n in mats}
        wrad = sb("w_radial", [P, D])
        bias = [sb(f"bias{l}", [1, W2]) for l in range(4)]
        bias_n = sb("bias_n", [P, D])
        be1c, be2c, bn1c, bac, alpha, nalpha = (sb(n, [P, 1]) for n in
                                                ("be1c", "be2c", "bn1c", "bac", "alpha", "nalpha"))

        ARENA = 20 * CW + 8 * CHUNK
        arena = sb("arena", [P, ARENA])
        used = [0]

        def part(n):
            used[0] += n
            assert used[0] <= ARENA, used[0]
            return arena[:, used[0] - n:used[0]]

        e_int = [part(4).bitcast(I32) for _ in range(RING)]
        e_sct = [part(2).bitcast(I32) for _ in range(RING)]
        e_flt = [part(8) for _ in range(RING)]
        e_meta = [part(8) for _ in range(RING)]
        e_rank = [part(2) for _ in range(RING)]
        e_att = [part(2) for _ in range(RING)]
        e_row = [[part(W2) for _ in range(RING)] for _ in range(2)]
        e_msg = [part(W2) for _ in range(RING)]
        e_eq = [part(2 * P) for _ in range(RING)]
        shared = [part(2 * W2) for _ in range(RING)]
        e_raw = [t[:, 0:W2] for t in shared]
        e_parts = [t[:, 0:D3].bitcast(BF16) for t in shared]
        e_T = [part(2 * P) for _ in range(2)]
        e_X = [t[:, W2:2 * W2] for t in shared]
        e_sig1 = [part(P) for _ in range(2)]
        e_sig2 = [part(P) for _ in range(2)]
        e_h1 = [part(P) for _ in range(2)]
        e_h2 = [part(P) for _ in range(2)]
        hot = [part(P + C).bitcast(F16) for _ in range(3)]
        junk = [[part(P) for _ in range(2)] for _ in range(2)]
        e_win = [part(WP).bitcast(BF16) for _ in range(3)]
        s_attr = part(GROUPS * P * 3)
        s_key = [part(GROUPS * P).bitcast(I32) for _ in range(2)]
        s_val = [part(GROUPS * P) for _ in range(3)]
        s_low, s_from = part(GROUPS), part(GROUPS)
        s_lowi = part(GROUPS).bitcast(I32)
        tmp = s_attr[:, 0:C]
        tmpi = [part(WP).bitcast(I32) for _ in range(2)]
        furthest, furthest1 = part(1), part(1)
        used[0] = 0
        n_x = [part(CW) for _ in range(NRING)]
        n_a = [[part(CW) for _ in range(2)] for _ in range(2)]
        n_b = part(CW)
        three = arena[:, used[0] - 3 * CW:used[0]]
        n_p = [three[:, k * 3 * CW // 2:(k + 1) * 3 * CW // 2].bitcast(BF16) for k in range(2)]
        n_p3 = [agg[:, k * 3 * CW // 2:(k + 1) * 3 * CW // 2].bitcast(BF16) for k in range(2)]
        n_T, n_y, n_r = ([part(CW) for _ in range(2)] for _ in range(3))
        n_q = [part(CW) for _ in range(NRING)]
        n_s = part(CW)
        root_, step_ = n_s[:, 0:C], n_s[:, C:2 * C]
        n_m, n_v = ([part(CHUNK) for _ in range(NRING)] for _ in range(2))

        f_int, f_tgt, f_flt, f_rank = e_int[0], e_sct[0], e_flt[0], e_rank[0]
        f_rows, f_msg, f_eq, f_junk = e_parts[0][:, 0:D3], e_msg[0][:, 0:D], e_eq[0].bitcast(BF16)[:, 0:P], junk[0][0]

        psum = ctx.enter_context(nc.psum_tensor("psum", [P, 8, 512], F32))
        p_hist = psum[:, 0, 0:C]
        p_key = [psum[:, 1 + k, :] for k in range(2)]
        p_sum = [psum[:, 3 + k, 0:W2] for k in range(2)]
        p_T = psum[:, 5, 0:2 * P]
        p_mlp = [psum[:, 6, 0:P], psum[:, 7, 0:P]]
        p_win = [psum[:, 5 + k, :] for k in range(3)]
        third = [slot % 2 for slot in range(RING - 1)] + [2]
        p_nat = psum[:, 0, 0:P + 2]
        p_set = [psum[:, 1 + k, 0:C] for k in range(4)]
        p_far = psum[0:1, 5, 0:P]
        flat = psum[:, :, :].rearrange("p b c -> p (b c)")
        p_nT = [flat[:, 2048 * 0 + 1024 * k:1024 * k + CW] for k in range(2)]
        p_nO = [flat[:, 2048 + 1024 * k:2048 + 1024 * k + CW] for k in range(2)]

        x_copied, edges_loaded, weights_loaded = sem("x_copied"), sem("edges_loaded"), sem("weights_loaded")
        pad_clear, iota_done, setup_step, degree_rooted = (sem(n) for n in
                                                       ("pad_clear", "iota_done", "setup_step", "degree_rooted"))
        zero_ready, zeroed = sem("zero_ready"), sem("zeroed")
        staged, unrolled, furthest_made, furthest_flipped, flag_ready = (
            sem(n) for n in ("staged", "unrolled", "furthest_made", "furthest_flipped", "flag_ready"))
        window_hot, window_summed, folded = sem("window_hot"), sem("window_summed"), sem("folded")
        f_ready, f_gathered, f_spread, f_step, f_equal, f_summed, f_message, f_added, f_back, pool_through = (
            sem(n) for n in ("f_ready", "f_gathered", "f_spread", "f_step", "f_equal", "f_summed", "f_message",
                             "f_added", "f_back", "pool_through"))
        high_kept, rest_made, middle_kept, low_made = (
            sem(n) for n in ("high_kept", "rest_made", "middle_kept", "low_made"))
        inverted = sem("inverted")
        x_in = [sem(f"x_in{k}") for k in range(NRING)]
        x_stored = [sem(f"x_stored{k}") for k in range(NRING)]
        scaled, agg_clear = sem("scaled"), sem("agg_clear")
        flipped, flip_copied = sem("flipped"), sem("flip_copied")
        squares = sem("attr_squares")
        meta_ready, onehot, counted = sem("meta_ready"), sem("onehot"), sem("counted")
        ranked, distance, target_made = sem("ranked"), sem("distance"), sem("target_made")
        rows_ready = sem("rows_ready")
        gathered = [sem(f"gathered{s}") for s in range(RING)]
        key_spread, equal, summed, msg_ready = (sem(n) for n in ("key_spread", "equal", "summed", "msg_ready"))
        added = [sem(f"added{k}") for k in range(2)]
        flipped_rows, rows_T, radial_term = sem("flipped_rows"), sem("rows_T"), sem("radial_term")
        mlp1, sig1, act1, mlp2, sig2, act2 = (sem(n) for n in ("mlp1", "sig1", "act1", "mlp2", "sig2", "act2"))
        natural, att_ready, weighted = sem("natural"), sem("att_ready"), sem("weighted")
        loaded = [sem(f"loaded{k}") for k in range(NRING)]
        agg_T, agg_T_kept, agg_out = sem("agg_T"), sem("agg_T_kept"), sem("agg_out")
        z_out, z_sig, z_ready = sem("z_out"), sem("z_sig"), sem("z_ready")
        rectified, x_new = sem("rectified"), sem("x_new")
        x_part, x_sum, var_sum, norm_step, mean_ready = (sem(n) for n in
                                                         ("x_part", "x_sum", "var_sum", "norm_step", "mean_ready"))
        centred, squared, var_ready, rstd_ready, h_ready = (sem(n) for n in
                                                            ("centred", "squared", "var_ready", "rstd_ready", "h_ready"))
        stored = [sem(f"stored{k}") for k in range(NRING)]
        out_stored = sem("out_stored")

        HALF = CHUNKS // NRING
        TOTAL = 16 * HALF

        counts_plus, hist_closed = sem("counts_plus"), sem("hist_closed")
        wait_over, wait_over_v, wait_over_s = sem("wait_over"), sem("wait_over_v"), sem("wait_over_s")
        meta_built, weights_clear = sem("meta_built"), sem("weights_clear")
        x_by_tile = x[0:NODE_TILES * P, :].rearrange("(t p) d -> p t d", p=P)
        out_by_tile = out[0:NODE_TILES * P, :].rearrange("(t p) d -> p t d", p=P)
        xs_by_tile = xs.rearrange("p (t d) -> p t d", d=D)

        def pair(t, j):
            return t[:, j * W2:(j + 1) * W2]

        def cols(c):
            return bass.ds(c * CHUNK, CHUNK)

        def spread(t, n):
            return t.unsqueeze(2).to_broadcast([P, n, D])

        def grid(t, n=CHUNK):
            return t.rearrange("p (t d) -> p t d", d=D) if len(t.shape) == 2 else t

        def agg_of(c):
            return agg[:, bass.ds(c * CW, CW)]

        SPLIT = {0: 0, 1: 1, 3: 2}

        def parts_of(n, slot, k):
            return (n_p3 if n == 3 else n_p)[slot % 2].rearrange("p (t d) -> p t d", d=D3)[:, :, k * D:(k + 1) * D]

        def last_use(q, slot):
            return q if slot == 0 else q - 1

        KEYED = {L0: 0, L1: 1, L3: 2}
        tables_in = [1, 1, 2, 1]
        gathers_before = [16 * 2 * (PAIRS // RING) * sum(tables_in[:l]) for l in range(4)]
        Z_PARTS = C * D // ZW
        ZEROED = 16 * 2 * (Z_PARTS + 1)
        X_PARTS = 13
        X_COPIES = 16 * (X_PARTS + 3)
        EDGE_LOADS = 16 * 3 * 3
        WEIGHT_LOADS = 16 * (2 * len(mats) + 2 + 1 + 8 + 1 + 6 + 2)
        STRAGGLER_ADDS = C + 2

        block = ctx.enter_context(nc.Block())

        @block.sync
        def _(sp):
            in_groups = (GROUPS - 1) * GP
            for tile, a, w in ((s_key[0], dst, 1), (s_key[1], src, 1), (s_attr, edge_attr, 3)):
                flat_ = a if w == 1 else a.rearrange("n d -> (n d)")
                T = P * w
                sp.dma_start(tile[0:GP, 0:(GROUPS - 1) * T].rearrange("p (k e) -> p k e", e=T),
                             flat_[0:in_groups * T].rearrange("(k p e) -> p k e", p=GP, e=T)
                             ).then_inc(edges_loaded, 16)
                last_rows = EDGE_TILES - in_groups
                sp.dma_start(tile[0:last_rows, (GROUPS - 1) * T:],
                             flat_[in_groups * T:EDGE_TILES * T].rearrange("(p e) -> p e", e=T)
                             ).then_inc(edges_loaded, 16)
            sp.wait_ge(pad_clear, 1)
            for tile, a, w in ((s_key[0], dst, 1), (s_key[1], src, 1), (s_attr, edge_attr, 3)):
                flat_ = a if w == 1 else a.rearrange("n d -> (n d)")
                T = P * w
                sp.dma_start(tile[last_rows:last_rows + 1, (GROUPS - 1) * T:(GROUPS - 1) * T + EDGE_REST * w],
                             flat_[EDGE_TILES * T:E * w].rearrange("(p e) -> p e", p=1)).then_inc(edges_loaded, 16)

            sp.wait_ge(zero_ready, 1)
            step = NODE_TILES // X_PARTS
            for k in range(X_PARTS):
                sp.dma_start(xs_by_tile[:, k * step:(k + 1) * step, :],
                             x_by_tile[:, k * step:(k + 1) * step, :]).then_inc(x_copied, 16)
            sp.dma_start(xs_by_tile[0:NODE_REST, NODE_TILES, :], x[NODE_TILES * P:N, :]).then_inc(x_copied, 16)
            sp.dma_start(xs_by_tile[NODE_REST:P, NODE_TILES, :], zero[0:P - NODE_REST, 0:D]).then_inc(x_copied, 16)
            sp.dma_start(xs_by_tile[:, NODE_TILES + 1, :], zero[:, 0:D]).then_inc(x_copied, 16)
            sp.wait_ge(x_copied, X_COPIES)
            sp.wait_ge(counts_plus, 1)

            for n in range(5):
                if n == 1:
                    sp.wait_ge(rows_ready, 1)
                    for a in acc:
                        with sp.Fori(0, Z_PARTS) as i:
                            sp.dma_start(by_partition(a)[:, bass.ds(i * ZW, ZW)], zero[:, :]).then_inc(zeroed, 16)
                        sp.dma_start(a[DUMP:DUMP + P, :], zero[:, 0:D]).then_inc(zeroed, 16)
                    sp.wait_ge(counts_plus, 2)
                if n:
                    if n - 1 == L2:
                        for k in range(2):
                            sp.wait_ge(added[k], 16 * PAIRS)
                    else:
                        sp.wait_ge(folded, 2 * PAIRS * (KEYED[n - 1] + 1))
                        sp.wait_ge(pool_through, KEYED[n - 1] + 1)
                    for s in range(NRING):
                        wait(sp, x_stored[s], TOTAL * (n - 1))

                def load_layer(c, slot, turn):
                    wait(sp, agg_T, 2 * CHUNKS + c)
                    for buf, a in ((n_a[0][slot % 2], acc[0]), (n_a[1][slot % 2], acc[1]), (n_b, table[L2])):
                        sp.dma_start(buf, by_partition(a)[:, bass.ds(c * CW, CW)]).then_inc(loaded[slot], 16)

                def load_x(c, slot, turn, n=n):
                    if not (isinstance(c, int) and c < NRING):
                        if n < 4:
                            sp.wait_ge(centred, n * CHUNKS + c - NRING + 1)
                            sp.sem_inc(wait_over_s, 1)
                        if n:
                            sp.wait_ge(x_stored[slot], TOTAL * (n - 1) + 16 * turn)
                        sp.sem_inc(wait_over_s, 1)
                    sp.dma_start(n_x[slot], xs[:, bass.ds(c * CW, CW)]).then_inc(x_in[slot], 16)

                def store_x(c, slot, turn, n=n):
                    sp.wait_ge(x_new, (n - 1) * CHUNKS + c + 1)
                    sp.sem_inc(wait_over_s, 1)
                    if n < 4:
                        sp.dma_start(xs[:, bass.ds(c * CW, CW)], n_x[slot]).then_inc(x_stored[slot], 16)
                        return
                    last_chunk = isinstance(c, int) and c == CHUNKS - 1
                    count_ = NODE_TILES - c * CHUNK if last_chunk else CHUNK
                    sp.dma_start(out_by_tile[:, bass.ds(c * CHUNK, count_), :],
                                 grid(n_x[slot])[:, 0:count_, :]).then_inc(x_stored[slot], 16)
                    if last_chunk:
                        sp.dma_start(out[NODE_TILES * P:N, :],
                                     grid(n_x[slot])[0:NODE_REST, count_, :]).then_inc(out_stored, 16)

                def store_rows(c, slot, turn, n=n):
                    if n == 2:
                        sp.wait_ge(h_ready, n * CHUNKS + c + 1)
                    else:
                        sp.wait_ge(low_made, SPLIT[n] * CHUNKS + c + 1)
                    sp.sem_inc(wait_over_s, 1)
                    wide = CHUNK * (D if n == 2 else D3)
                    sp.dma_start(by_partition(table[n])[:, bass.ds(c * wide, wide)],
                                 n_q[slot] if n == 2 else (n_p3 if n == 3 else n_p)[slot % 2]
                                 ).then_inc(stored[slot], 16)

                lag = 2 if n else 1
                pipeline(sp, CHUNKS, NRING, ([(0, load_layer)] if n == 3 else []) +
                         ([(3, store_x)] if n else []) + [(0, load_x)] +
                         ([(lag + (2 if n == 2 else 4), store_rows)] if n < 4 else []))
            sp.wait_ge(out_stored, 16)
            for s in range(NRING):
                sp.wait_ge(x_stored[s], TOTAL * 4)

        @block.gpsimd
        def _(pool):
            nc.gpsimd.iota(tmpi[0], [[1, WP]], base=0, channel_multiplier=0)
            nc.gpsimd.iota(e_int[0][:, 0:1], [[0, 1]], base=0, channel_multiplier=1)
            nc.gpsimd.iota(e_int[0][:, 1:2], [[0, 1]], base=DUMP, channel_multiplier=1)
            nc.gpsimd.memset(expo[:, :], -0.5).then_inc(iota_done, 1)

            for n in range(5):
                def centre(c, slot, turn, n=n):
                    pool.wait_ge(mean_ready, n * CHUNKS + c + 1)
                    if not (isinstance(c, int) and c < NRING):
                        if n == 2:
                            pool.wait_ge(stored[slot], TOTAL * n + 16 * turn)
                        else:
                            pool.wait_ge(low_made, SPLIT[n] * CHUNKS + c - NRING + 1)
                    nc.gpsimd.tensor_tensor(grid(n_q[slot]), grid(n_x[slot]), spread(n_m[slot], CHUNK),
                                            ALU.subtract).then_inc(centred, 1)

                def rest_of(c, slot, turn, n=n):
                    pool.wait_ge(high_kept, SPLIT[n] * CHUNKS + c + 1)
                    nc.gpsimd.tensor_tensor(grid(n_q[slot]), grid(n_q[slot] if n == 3 else agg_of(c)),
                                            parts_of(n, slot, 0), ALU.subtract).then_inc(rest_made, 1)

                def low(c, slot, turn, n=n):
                    pool.wait_ge(middle_kept, SPLIT[n] * CHUNKS + c + 1)
                    nc.gpsimd.tensor_tensor(parts_of(n, slot, 2), grid(n_q[slot]), parts_of(n, slot, 1),
                                            ALU.subtract).then_inc(low_made, 1)

                def rstd(c, slot, turn):
                    pool.wait_ge(var_ready, 3 * CHUNKS + c + 1)
                    nc.gpsimd.tensor_tensor(n_v[slot], n_v[slot], expo[:, 0:1].to_broadcast([P, CHUNK]),
                                            ALU.pow).then_inc(rstd_ready, 1)

                if n < 4:
                    lag = 2 if n else 1
                    pipeline(pool, CHUNKS, NRING, ([(lag + 4, low), (lag + 3, rest_of)] if n in SPLIT else []) +
                             [(lag, centre)] + ([(lag + 1, rstd)] if n == 3 else []))
                if n < 4:
                    l = n

                    def gather(q, slot, turn, l=l):
                        pool.wait_ge(rows_ready, l * PAIRS + q + 1)
                        pool.sem_inc(wait_over, 1)
                        for k in range(tables_in[l]):
                            for j in range(2):
                                to = (e_row[k][slot][:, j * D:(j + 1) * D] if l == L2 else
                                      e_parts[slot][:, j * D3:(j + 1) * D3])
                                nc.gpsimd.indirect_dma_start(
                                    out=to, out_offset=None, in_=table[l][:, :],
                                    in_offset=bass.IndirectOffsetOnAxis(
                                        ap=e_int[slot][:, 2 * k + j:2 * k + j + 1], axis=0),
                                ).then_inc(gathered[slot], 16)

                    def add(q, slot, turn):
                        pool.wait_ge(msg_ready, q + 1)
                        pool.wait_ge(target_made, q + 1)
                        for j in range(2):
                            wait(pool, added[j], 16 * q)
                            pool.sem_inc(wait_over, 1)
                            nc.gpsimd.indirect_dma_start(
                                out=acc[j][:, :],
                                out_offset=bass.IndirectOffsetOnAxis(ap=e_sct[slot][:, j:j + 1], axis=0),
                                in_=e_msg[slot][:, j * D:(j + 1) * D], in_offset=None,
                                compute_op=ALU.add).then_inc(added[j], 16)

                    if l == L2:
                        pool.wait_ge(zeroed, ZEROED)
                        pipeline(pool, PAIRS, RING, [(0, gather), (4, add)])
                        continue
                    pipeline(pool, PAIRS, RING, [(0, gather)])

                    if l == L0:
                        pool.wait_ge(flag_ready, 1)
                        any_missed = pool.value_load(flag[0:1, 0:1], min_val=0, max_val=1)
                    w = KEYED[l]
                    with pool.If(any_missed > 0):
                        pool.wait_ge(folded, 2 * PAIRS * (w + 1))
                        pool.dma_start(by_partition(acc_s), agg[:, :]).then_inc(f_added, 16)
                        pool.dma_start(acc_s[DUMP:DUMP + P, :], zero[:, 0:D]).then_inc(f_added, 16)
                        with pool.Fori(0, C) as a:
                            pool.wait_ge(f_ready, w * C + a + 1)
                            pool.sem_inc(wait_over, 1)
                            nc.gpsimd.indirect_dma_start(
                                out=f_rows, out_offset=None, in_=table[l][:, :],
                                in_offset=bass.IndirectOffsetOnAxis(ap=f_int[:, 0:1], axis=0),
                            ).then_inc(f_gathered, 16)
                            pool.wait_ge(f_message, w * C + a + 1)
                            pool.sem_inc(wait_over, 1)
                            nc.gpsimd.indirect_dma_start(
                                out=acc_s[:, :], out_offset=bass.IndirectOffsetOnAxis(ap=f_tgt[:, 0:1], axis=0),
                                in_=f_msg, in_offset=None, compute_op=ALU.add).then_inc(f_added, 16)
                        pool.wait_ge(f_added, 16 * STRAGGLER_ADDS * (w + 1))
                        pool.dma_start(agg[:, :], by_partition(acc_s)).then_inc(f_back, 16)
                        pool.wait_ge(f_back, 16 * (w + 1))
                    pool.sem_inc(pool_through, 1)

        @block.scalar
        def _(act):
            def load(dst_, src_):
                act.dma_start(dst_, src_).then_inc(weights_loaded, 16)

            act.wait_ge(edges_loaded, EDGE_LOADS)
            nc.scalar.activation(s_attr[0:GP, :], s_attr[0:GP, :], ACT.Square).then_inc(squares, 1)
            act.wait_ge(weights_clear, 1)
            blocks = {"W0": W0, "W1": W1, "W3": W3, "We1s": We1[0:D, :], "We1d": We1[D:2 * D, :], "We2": We2,
                      "Wn1h": Wn1[D - D:D, :], "Wn1a": Wn1[D:2 * D, :], "Wn2": Wn2}
            for name in mats:
                for h in range(2):
                    load(bd[name][h * D:(h + 1) * D, h * D:(h + 1) * D], blocks[name])
            for h in range(2):
                load(ext[h * D:(h + 1) * D, P + h:P + h + 1], Wa)
            load(wrad[:, :], We1[2 * D:2 * D + 1, :].to_broadcast([P, D]))
            for l, b in enumerate((b0, b1, bn2, b3)):
                for h in range(2):
                    load(bias[l][:, h * D:(h + 1) * D], b.rearrange("(o d) -> o d", o=1))
            load(bias_n[:, :], bn2.rearrange("(o d) -> o d", o=1).to_broadcast([P, D]))
            for t, b in ((be1c, be1), (be2c, be2), (bn1c, bn1)):
                for h in range(2):
                    load(t[h * D:(h + 1) * D, :], b.rearrange("(d o) -> d o", o=1))
            for t, b in ((bac, ba), (alpha, prelu_a)):
                load(t[:, :], b.rearrange("(o d) -> o d", o=1).to_broadcast([P, 1]))

            def index_load(k):
                def stage(q, slot, turn):
                    wait(act, counted, k * PAIRS + q - RING + 1)
                    nc.scalar.copy(e_meta[slot].rearrange("p (a b) -> p a b", b=4),
                                   meta[k][:, bass.ds(2 * q, 2), :]).then_inc(meta_ready, 1)
                return stage

            act.wait_ge(meta_built, 1)
            pipeline(act, PAIRS, RING, [(0, index_load(0))])

            def degree_root(k):
                act.wait_ge(counts_plus, k + 1)
                nc.scalar.activation(root_, dinv[k][:, :], ACT.Sqrt).then_inc(degree_rooted, 1)

            degree_root(0)
            for n in range(5):
                def keep_T(c, slot, turn, n=n):
                    g = (n - 1) * CHUNKS + c
                    act.wait_ge(agg_T, g + 1)
                    if n == 3:
                        wait(act, z_out, c - 1)
                    else:
                        wait(act, agg_out, g - 1)
                    last = nc.scalar.copy(n_T[slot % 2], p_nT[0 if n == 3 else slot % 2])
                    if n == 3:
                        last = nc.scalar.copy(n_y[slot % 2], p_nT[1])
                    last.then_inc(agg_T_kept, 1)

                def rectify(c, slot, turn):
                    act.wait_ge(agg_out, c + 1)
                    wait(act, x_new, c - 1)
                    nc.scalar.activation(n_r[slot % 2], p_nO[slot % 2], ACT.Relu, scale=-1.0)
                    nc.scalar.activation(n_y[slot % 2], p_nO[slot % 2], ACT.Relu).then_inc(rectified, 1)

                def z_sigmoid(c, slot, turn):
                    act.wait_ge(z_out, c + 1)
                    wait(act, agg_out, 2 * CHUNKS + c - 1)
                    nc.scalar.activation(n_r[slot % 2], p_nO[0], ACT.Sigmoid, bias=bn1c[:, 0:1]).then_inc(z_sig, 1)

                def square(c, slot, turn, n=n):
                    act.wait_ge(centred, n * CHUNKS + c + 1)
                    wait(act, var_ready, n * CHUNKS + c)
                    nc.scalar.activation(n_s, n_q[slot], ACT.Square).then_inc(squared, 1)

                def root(c, slot, turn, n=n):
                    act.wait_ge(var_ready, n * CHUNKS + c + 1)
                    nc.scalar.activation(n_v[slot], n_v[slot], ACT.Sqrt).then_inc(rstd_ready, 1)

                def high(c, slot, turn, n=n):
                    act.wait_ge(h_ready, n * CHUNKS + c + 1)
                    if not (isinstance(c, int) and c < 2):
                        act.wait_ge(stored[(slot + 2) % NRING], TOTAL * n + 16 * (turn + (1 if slot >= 2 else 0)))
                    nc.scalar.copy(parts_of(n, slot, 0), grid(n_q[slot] if n == 3 else agg_of(c))
                                   ).then_inc(high_kept, 1)

                def middle(c, slot, turn, n=n):
                    act.wait_ge(rest_made, SPLIT[n] * CHUNKS + c + 1)
                    nc.scalar.copy(parts_of(n, slot, 1), grid(n_q[slot])).then_inc(middle_kept, 1)

                lag = 2 if n else 1
                stages = [(1, keep_T)] if n == 3 else []
                if n < 3:
                    stages.append((lag + 2, root))
                if n == 1:
                    stages.append((2, rectify))
                if n < 4:
                    stages.append((lag + 1, square))
                if n in SPLIT:
                    stages += [(lag + 3, middle), (lag + 2, high)]
                if n in (1, 2, 4):
                    stages.append((0, keep_T))
                if n == 3:
                    stages.append((1, z_sigmoid))
                pipeline(act, CHUNKS, NRING, stages)
                if n == 4:
                    break

                l = n
                for s in range(NRING):
                    wait(act, x_stored[s], TOTAL * l)
                    act.wait_ge(stored[s], TOTAL * (l + 1))

                def rows(q, slot, turn, l=l):
                    two = bass.ds(2 * q, 2)
                    if l == L2:
                        for j in range(2):
                            wait(act, added[j], 16 * (q - RING + 1))
                    elif not (isinstance(q, int) and q < RING):
                        act.wait_ge(window_summed, KEYED[l] * PAIRS + q - RING + 1)
                    nc.scalar.copy(e_int[slot][:, 0:2], index[1][:, two])
                    if l == L2:
                        nc.scalar.copy(e_int[slot][:, 2:4], index[0][:, two])
                        nc.scalar.copy(e_flt[slot][:, 4:6], radial[:, two])
                        last = nc.scalar.copy(e_flt[slot][:, 0:4].rearrange("p (a b) -> p a b", b=2),
                                              meta[1][:, two, 0:2])
                    else:
                        last = nc.scalar.copy(e_flt[slot][:, 0:2], krel[:, two])
                    last.then_inc(rows_ready, 1)

                def message(q, slot, turn):
                    act.wait_ge(summed, q + 1)
                    nc.scalar.copy(e_msg[slot], p_sum[slot % 2]).then_inc(msg_ready, 1)

                def keep_rows_T(q, slot, turn):
                    act.wait_ge(flipped_rows, q + 1)
                    wait(act, mlp1, last_use(q, slot))
                    nc.scalar.copy(e_T[slot % 2], p_T).then_inc(rows_T, 1)

                def sigmoid1(q, slot, turn):
                    act.wait_ge(mlp1, q + 1)
                    wait(act, act1, last_use(q, slot))
                    nc.scalar.activation(e_sig1[slot % 2], p_mlp[0], ACT.Sigmoid,
                                         bias=be1c[:, 0:1]).then_inc(sig1, 1)

                def sigmoid2(q, slot, turn):
                    act.wait_ge(mlp2, q + 1)
                    wait(act, act2, last_use(q, slot))
                    nc.scalar.activation(e_sig2[slot % 2], p_mlp[1], ACT.Sigmoid,
                                         bias=be2c[:, 0:1]).then_inc(sig2, 1)

                def attention(q, slot, turn):
                    act.wait_ge(natural, q + 1)
                    nc.scalar.activation(e_att[slot], p_nat[:, P:P + 2], ACT.Sigmoid,
                                         bias=bac[:, 0:1]).then_inc(att_ready, 1)

                if l == L2:
                    pipeline(act, PAIRS, RING, [(0, rows), (2, keep_rows_T), (3, sigmoid2), (2, sigmoid1),
                                                (3, attention), (3, message)])
                elif l == L0:
                    pipeline(act, PAIRS, RING, [(0, rows), (0, index_load(1))])
                    degree_root(1)
                else:
                    pipeline(act, PAIRS, RING, [(0, rows)])

        @block.vector
        def _(dve):
            tail = 96
            for t in s_key:
                nc.vector.memset(t[tail:GP, (GROUPS - 1) * P:], P * C - 1)
            nc.vector.memset(s_attr[tail:GP, (GROUPS - 1) * P * 3:], 0.0).then_inc(pad_clear, 1)
            for name in mats:
                nc.vector.memset(bd[name][:, :], 0.0)
            nc.vector.memset(ext[:, P:P + 2], 0.0).then_inc(weights_clear, 1)
            nc.vector.memset(ones[:, :], 1.0)
            nc.vector.memset(zero[:, :], 0.0).then_inc(zero_ready, 1)

            link = linker(dve, setup_step, 0)
            dve.wait_ge(iota_done, 1)
            link(nc.vector.tensor_copy(colf[:, :], tmpi[0][:, 0:P]))
            link(nc.vector.tensor_copy(col16[:, :], tmpi[0]))
            link(nc.vector.tensor_copy(pcol[:, :], e_int[0][:, 0:1]))
            link(nc.vector.tensor_copy(dumprow[:, :], e_int[0][:, 1:2]))
            nc.vector.tensor_scalar(ident, colf[:, :], pcol[:, 0:1], None, ALU.is_equal)
            nc.vector.tensor_scalar(tri[:, :], colf[:, :], pcol[:, 0:1], None, ALU.is_lt)

            dve.wait_ge(edges_loaded, EDGE_LOADS)
            nc.vector.tensor_copy(s_val[1][0:GP, :], s_key[1][0:GP, :])
            link(nc.vector.tensor_copy(s_val[0][0:GP, :], s_key[0][0:GP, :]))
            low, lowi, start = s_low[0:GP, :], s_lowi[0:GP, :], s_from[0:GP, :]
            link(nc.vector.tensor_reduce(low, s_val[0][0:GP, :].rearrange("p (k e) -> p k e", e=P), axis=AX.X,
                                         op=ALU.min))
            link(nc.vector.tensor_copy(lowi, low))
            link(nc.vector.tensor_scalar(lowi, lowi, SHIFT, None, ALU.arith_shift_right))
            link(nc.vector.tensor_copy(start, lowi))
            link(nc.vector.tensor_scalar(start, start, float(C - WIN), None, ALU.min))
            dve.wait_ge(squares, 1)
            nc.vector.tensor_reduce(s_val[2][0:GP, :], s_attr[0:GP, :].rearrange("p (t d) -> p t d", d=3),
                                    axis=AX.X, op=ALU.add).then_inc(staged, 1)

            dve.wait_ge(unrolled, 1)
            for k in range(2):
                row, dist, part_, col = (meta[k][:, :, j] for j in range(4))
                raw, bits = tmpi[0][:, 0:C], tmpi[1][:, 0:C]
                link(nc.vector.tensor_copy(raw, p_set[k]))
                link(nc.vector.tensor_scalar(bits, raw, P - 1, None, ALU.bitwise_and))
                link(nc.vector.tensor_copy(part_, bits))
                link(nc.vector.tensor_scalar(bits, raw, SHIFT, None, ALU.arith_shift_right))
                link(nc.vector.tensor_copy(col, bits))
                link(nc.vector.scalar_tensor_tensor(out=row, in0=part_, scalar=float(C), in1=col,
                                                    op0=ALU.mult, op1=ALU.add))
                link(nc.vector.tensor_copy(index[k][:, :], row))
                link(nc.vector.tensor_scalar(dist, row, dumprow[:, 0:1], None, ALU.subtract))
            link(nc.vector.tensor_tensor(krel[:, :], meta[0][:, :, 3], p_set[3], ALU.subtract))
            link(nc.vector.scalar_tensor_tensor(out=krel[:, :], in0=krel[:, :], scalar=float(P),
                                                in1=meta[0][:, :, 2], op0=ALU.mult, op1=ALU.add))
            link(nc.vector.scalar_tensor_tensor(out=missed[:, :], in0=krel[:, :], scalar=float(WP),
                                                in1=meta[0][:, :, 1], op0=ALU.is_ge, op1=ALU.mult))
            link(nc.vector.tensor_scalar(tmp, p_set[3], float(D), None, ALU.mult))
            link(nc.vector.tensor_copy(window[:, :], tmp))
            nc.vector.tensor_copy(radial[:, :], p_set[2]).then_inc(meta_built, 1)
            nc.vector.tensor_reduce(furthest, krel[:, :], axis=AX.X, op=ALU.max).then_inc(furthest_made, 1)
            dve.wait_ge(furthest_flipped, 1)
            link(nc.vector.tensor_reduce(furthest1[0:1, :], p_far, axis=AX.X, op=ALU.max))
            link(nc.vector.tensor_scalar(furthest1[0:1, :], furthest1[0:1, :], float(WP), None, ALU.is_ge))
            nc.vector.tensor_copy(flag[:, :], furthest1[0:1, :]).then_inc(flag_ready, 1)

            def one_hots(k):
                def stage(q, slot, turn):
                    g = k * PAIRS + q
                    dve.wait_ge(meta_ready, g + 1)
                    wait(dve, counted, k * PAIRS + q - 1)
                    buf = hot[third[slot]]
                    for j in range(2):
                        nc.vector.tensor_scalar(buf[:, j * P:(j + 1) * P], col16[:, 0:P],
                                                e_meta[slot][:, 4 * j + 2:4 * j + 3], None, ALU.is_equal)
                        last = nc.vector.tensor_scalar(buf[:, 2 * P + j * C:2 * P + (j + 1) * C], col16[:, 0:C],
                                                       e_meta[slot][:, 4 * j + 3:4 * j + 4], None, ALU.is_equal)
                    last.then_inc(onehot, 1)
                return stage

            def finalise(k):
                dve.wait_ge(hist_closed, k + 1)
                last = nc.vector.tensor_scalar(dinv[k][:, :], p_hist, 1.0, None, ALU.add)
                last.then_inc(counts_plus, 1)
                if k == 0:
                    link(nc.vector.tensor_scalar(rdeg[:, :], p_hist, 1.0, None, ALU.max))
                    link(nc.vector.reciprocal(rdeg[:, :], rdeg[:, :]))

            pipeline(dve, PAIRS, RING, [(0, one_hots(0))])
            finalise(0)
            dve.wait_ge(weights_loaded, WEIGHT_LOADS)
            for m, name in enumerate(("W0", "W3")):
                dve.wait_ge(flipped, 2)
                nc.vector.tensor_copy(bd[name][:, :], p_sum[m])
            nc.vector.tensor_scalar(nalpha[:, :], alpha[:, :], -1.0, None, ALU.mult).then_inc(flip_copied, 1)
            dve.wait_ge(flip_copied, 1)

            for n in range(5):
                def scale(c, slot, turn, n=n):
                    factor = {1: dinv[0], 2: dinv[1], 4: rdeg}[n]
                    wait(dve, agg_T, (n - 1) * CHUNKS + c - 1)
                    nc.vector.tensor_tensor(grid(n_a[0][slot % 2]), grid(agg_of(c)),
                                            spread(factor[:, cols(c)], CHUNK), ALU.mult).then_inc(scaled, 1)

                def combine(c, slot, turn):
                    dve.wait_ge(loaded[slot], 16 * 3 * (turn + 1))
                    nc.vector.tensor_tensor(n_a[0][slot % 2], n_a[0][slot % 2], n_a[1][slot % 2],
                                            ALU.add).then_inc(scaled, 1)

                def activate_z(c, slot, turn):
                    dve.wait_ge(z_sig, c + 1)
                    nc.vector.scalar_tensor_tensor(out=n_r[slot % 2], in0=p_nO[0], scalar=bn1c[:, 0:1],
                                                   in1=n_r[slot % 2], op0=ALU.add,
                                                   op1=ALU.mult).then_inc(z_ready, 1)

                def residual(c, slot, turn, n=n):
                    g = (n - 1) * CHUNKS + c
                    xc = n_x[slot]
                    dve.wait_ge(x_in[slot], TOTAL * n + 16 * (turn + 1))
                    if n == 1:
                        dve.wait_ge(rectified, c + 1)
                        nc.vector.tensor_tensor(xc, xc, n_y[slot % 2], ALU.add).then_inc(x_part, 1)
                        dve.wait_ge(x_part, c + 1)
                        nc.vector.scalar_tensor_tensor(out=xc, in0=n_r[slot % 2], scalar=nalpha[:, 0:1], in1=xc,
                                                       op0=ALU.mult, op1=ALU.add).then_inc(x_new, 1)
                    elif n == 3:
                        dve.wait_ge(agg_out, g + 1)
                        nc.vector.tensor_tensor(xc, xc, p_nO[1], ALU.add).then_inc(x_part, 1)
                        dve.wait_ge(x_part, CHUNKS + c + 1)
                        nc.vector.tensor_tensor(grid(xc), grid(xc), bias_n[:, :].unsqueeze(1).to_broadcast(
                            [P, CHUNK, D]), ALU.add).then_inc(x_new, 1)
                    elif n:
                        dve.wait_ge(agg_out, g + 1)
                        nc.vector.tensor_tensor(xc, xc, p_nO[slot % 2], ALU.add).then_inc(x_new, 1)
                    if n == 4:
                        return
                    if n:
                        dve.wait_ge(x_new, g + 1)
                    dve.sem_inc(wait_over_v, 1)
                    nc.vector.tensor_reduce(n_m[slot], grid(xc), axis=AX.X, op=ALU.add).then_inc(x_sum, 1)
                    dve.wait_ge(x_sum, n * CHUNKS + c + 1)
                    nc.vector.tensor_scalar(n_m[slot], n_m[slot], 1.0 / D, None, ALU.mult).then_inc(mean_ready, 1)

                def variance(c, slot, turn, n=n):
                    g = n * CHUNKS + c
                    dve.wait_ge(squared, g + 1)
                    dve.sem_inc(wait_over_v, 1)
                    nc.vector.tensor_reduce(n_v[slot], grid(n_s), axis=AX.X, op=ALU.add).then_inc(var_sum, 1)
                    dve.wait_ge(var_sum, g + 1)
                    nc.vector.tensor_scalar(n_v[slot], n_v[slot], 1.0 / D, EPS, ALU.mult,
                                            ALU.add).then_inc(var_ready, 1)

                def normalise(c, slot, turn, n=n):
                    g = n * CHUNKS + c
                    link = linker(dve, norm_step, {0: c * 2, 1: c * 2 + 2 * CHUNKS, 2: c + 4 * CHUNKS, 3: 0}[n])
                    dve.wait_ge(rstd_ready, g + 1)
                    if n < 3:
                        link(nc.vector.reciprocal(n_v[slot], n_v[slot]))
                    if n < 2:
                        link(nc.vector.tensor_tensor(n_v[slot], n_v[slot], dinv[n][:, cols(c)], ALU.mult))
                    nc.vector.scalar_tensor_tensor(out=grid(agg_of(c)) if n < 2 else grid(n_q[slot]),
                                                   in0=grid(n_q[slot]), scalar=0.0,
                                                   in1=spread(n_v[slot], CHUNK), op0=ALU.max,
                                                   op1=ALU.mult).then_inc(h_ready, 1)

                if n < 2:
                    dve.wait_ge(degree_rooted, n + 1)
                    link = linker(dve, inverted, 5 * n)
                    link(nc.vector.reciprocal(root_, root_))
                    link(nc.vector.tensor_tensor(step_, root_, root_, ALU.mult))
                    link(nc.vector.tensor_tensor(step_, step_, dinv[n][:, :], ALU.mult))
                    link(nc.vector.tensor_scalar(step_, step_, -0.5, 1.5, ALU.mult, ALU.add))
                    link(nc.vector.tensor_tensor(dinv[n][:, :], root_, step_, ALU.mult))
                if n - 1 in KEYED:
                    dve.wait_ge(pool_through, KEYED[n - 1] + 1)
                lag = 2 if n else 1
                stages = [(0, combine if n == 3 else scale)] if n else []
                if n < 4:
                    stages.append((lag + 2, normalise))
                stages.append((lag, residual))
                if n < 4:
                    stages.append((lag + 1, variance))
                if n == 3:
                    stages.append((1, activate_z))
                pipeline(dve, CHUNKS, NRING, stages)
                if n == 4:
                    break

                l = n

                def window_one_hots(q, slot, l=l):
                    g = KEYED[l] * PAIRS + q
                    dve.wait_ge(rows_ready, l * PAIRS + q + 1)
                    if not (isinstance(g, int) and g < 2):
                        dve.wait_ge(window_summed, g - 1)
                    for j in range(2):
                        last = nc.vector.tensor_scalar(e_win[third[slot]][:, j * WP:(j + 1) * WP], col16[:, :],
                                                       e_flt[slot][:, j:j + 1], None, ALU.is_equal)
                    last.then_inc(window_hot, 1)

                def fold(q, slot, starts, between=None, l=l):
                    g = KEYED[l] * PAIRS + q
                    dve.wait_ge(window_summed, g + 1)
                    for j in range(2):
                        if j and between:
                            between()
                        if not (isinstance(g, int) and 2 * g + j == 0):
                            dve.wait_ge(folded, 2 * g + j)
                        at = agg[:, bass.ds(starts[2 * slot + j], WD)]
                        nc.vector.tensor_tensor(at, at, p_win[third[slot]][:, j * WD:(j + 1) * WD],
                                                ALU.add).then_inc(folded, 1)

                def turn_of(t, hot_stage=None, final=False):
                    starts = nc.values_load_multi_w_load_instructions(
                        window[0:1, bass.ds(t * (2 * RING), 2 * RING)], engines=(mybir.EngineType.DVE,), min_val=0,
                        max_val=(C - WIN) * D,
                        skip_runtime_bounds_check_because="the set-up keeps every start within 0..(C - WIN) * D")[1]
                    for s in range(RING):
                        if not (final and s == RING - 1):
                            window_one_hots(t * RING + s + 1, (s + 1) % RING)
                        fold(t * RING + s, s, starts,
                             (lambda s=s: hot_stage(t * RING + s, s, t)) if hot_stage else None)

                def stragglers(l=l):
                    w = KEYED[l]
                    with dve.Fori(0, C) as a:
                        g = w * C + a
                        dve.wait_ge(f_added, 16 * (w * STRAGGLER_ADDS + 2) + 16 * a)
                        nc.vector.tensor_copy(f_int[:, 0:1], index[1][:, bass.ds(a, 1)])
                        nc.vector.tensor_copy(f_flt[:, 1:2], missed[:, bass.ds(a, 1)]).then_inc(f_step, 1)
                        dve.wait_ge(f_step, 3 * g + 1)
                        nc.vector.tensor_scalar(f_flt[:, 0:1], f_flt[:, 1:2], dumprow[:, 0:1], None,
                                                ALU.add).then_inc(f_ready, 1)
                        dve.wait_ge(f_spread, g + 1)
                        nc.vector.scalar_tensor_tensor(
                            out=f_junk, in0=p_key[0][:, 0:P], scalar=f_flt[:, 0:1], in1=tri[:, :],
                            op0=ALU.is_equal, op1=ALU.mult, accum_out=f_rank[:, 0:1]).then_inc(f_step, 1)
                        nc.vector.tensor_scalar(f_eq, p_key[0][:, 0:P], f_flt[:, 0:1], None,
                                                ALU.is_equal).then_inc(f_equal, 1)
                        dve.wait_ge(f_step, 3 * g + 2)
                        nc.vector.scalar_tensor_tensor(
                            out=f_rank[:, 0:1], in0=f_rank[:, 0:1], scalar=0.0, in1=f_flt[:, 1:2],
                            op0=ALU.is_equal, op1=ALU.mult).then_inc(f_step, 1)
                        dve.wait_ge(f_step, 3 * g + 3)
                        nc.vector.tensor_scalar(f_tgt[:, 0:1], f_rank[:, 0:1], dumprow[:, 0:1], None, ALU.add)
                        dve.wait_ge(f_summed, g + 1)
                        nc.vector.tensor_copy(f_msg, p_sum[0][:, 0:D]).then_inc(f_message, 1)

                def equality(q, slot, turn):
                    dve.wait_ge(key_spread, q + 1)
                    keys = [p_key[slot % 2][:, j * P:(j + 1) * P] for j in range(2)]
                    for j in range(2):
                        last = nc.vector.scalar_tensor_tensor(
                            out=junk[slot % 2][j], in0=keys[j], scalar=e_flt[slot][:, 2 * j:2 * j + 1],
                            in1=tri[:, :], op0=ALU.is_equal, op1=ALU.mult, accum_out=e_rank[slot][:, j:j + 1])
                    last.then_inc(ranked, 1)
                    for j in range(2):
                        last = nc.vector.tensor_scalar(e_eq[slot][:, j * P:(j + 1) * P], keys[j],
                                                       e_flt[slot][:, 2 * j:2 * j + 1], None, ALU.is_equal)
                    last.then_inc(equal, 1)
                    dve.wait_ge(ranked, q + 1)
                    nc.vector.scalar_tensor_tensor(
                        out=e_rank[slot], in0=e_rank[slot], scalar=0.0, in1=e_flt[slot][:, 1:4:2],
                        op0=ALU.is_equal, op1=ALU.mult).then_inc(distance, 1)
                    dve.wait_ge(distance, q + 1)
                    nc.vector.tensor_scalar(e_sct[slot], e_rank[slot], dumprow[:, 0:1], None,
                                            ALU.add).then_inc(target_made, 1)

                def radial_part(q, slot, turn):
                    dve.wait_ge(rows_ready, L2 * PAIRS + q + 1)
                    nc.vector.tensor_tensor(grid(e_X[slot]), wrad[:, :].unsqueeze(1).to_broadcast([P, 2, D]),
                                            spread(e_flt[slot][:, 4:6], 2), ALU.mult).then_inc(radial_term, 1)

                def silu1(q, slot, turn):
                    dve.wait_ge(sig1, q + 1)
                    wait(dve, mlp2, last_use(q, slot))
                    nc.vector.scalar_tensor_tensor(out=e_h1[slot % 2], in0=p_mlp[0], scalar=be1c[:, 0:1],
                                                   in1=e_sig1[slot % 2], op0=ALU.add,
                                                   op1=ALU.mult).then_inc(act1, 1)

                def silu2(q, slot, turn):
                    dve.wait_ge(sig2, q + 1)
                    wait(dve, natural, last_use(q, slot))
                    nc.vector.scalar_tensor_tensor(out=e_h2[slot % 2], in0=p_mlp[1], scalar=be2c[:, 0:1],
                                                   in1=e_sig2[slot % 2], op0=ALU.add,
                                                   op1=ALU.mult).then_inc(act2, 1)

                def weigh(q, slot, turn):
                    dve.wait_ge(att_ready, q + 1)
                    nc.vector.tensor_tensor(grid(e_raw[slot]), grid(p_nat[:, 0:P]), spread(e_att[slot], 2),
                                            ALU.mult).then_inc(weighted, 1)

                if l == L2:
                    nc.vector.memset(agg[:, 3 * CW:], 0.0)
                    pipeline(dve, PAIRS, RING, [(0, equality), (0, radial_part), (1, silu2), (0, silu1),
                                                (1, weigh)])
                    continue
                if l == L0:
                    dve.wait_ge(flag_ready, 1)
                    any_missed = dve.value_load(flag[0:1, 0:1], min_val=0, max_val=1)
                if l == L3:
                    dve.wait_ge(rows_ready, L3 * PAIRS + 1)
                    nc.vector.memset(agg[:, 0:3 * CW], 0.0).then_inc(agg_clear, 1)
                    dve.wait_ge(agg_clear, 1)
                hot_stage = one_hots(1) if l == L0 else None
                window_one_hots(0, 0)
                turn_of(0, hot_stage)
                with dve.Fori(1, PAIRS // RING - 1) as t:
                    turn_of(t, hot_stage)
                turn_of(PAIRS // RING - 1, hot_stage, final=True)
                if l == L0:
                    finalise(1)
                dve.wait_ge(folded, 2 * PAIRS * (KEYED[l] + 1))
                with dve.If(any_missed > 0):
                    stragglers()

        @block.tensor
        def _(pe):
            def open_counts(k):
                nc.tensor.matmul(p_hist, zero[:, 0:P], zero[:, 0:C], start=True, stop=False)

            def close_counts():
                nc.tensor.matmul(p_hist, zero[:, 0:P], zero[:, 0:C], start=False,
                                 stop=True).then_inc(hist_closed, 1)

            def count(k):
                def stage(q, slot, turn):
                    pe.wait_ge(onehot, k * PAIRS + q + 1)
                    for j in range(2):
                        last = nc.tensor.matmul(p_hist, hot[third[slot]][:, j * P:(j + 1) * P],
                                                hot[third[slot]][:, 2 * P + j * C:2 * P + (j + 1) * C],
                                                start=False, stop=False)
                    last.then_inc(counted, 1)
                return stage

            pe.wait_ge(staged, 1)
            for k in range(GROUPS):
                for v in range(3):
                    nc.tensor.transpose(p_set[v][:, k * GP:(k + 1) * GP], s_val[v][0:GP, k * P:(k + 1) * P],
                                        ident[0:GP, 0:GP])
                last = nc.tensor.transpose(p_set[3][:, k * GP:(k + 1) * GP],
                                           s_from[0:GP, k:k + 1].to_broadcast([GP, P]), ident[0:GP, 0:GP])
            last.then_inc(unrolled, 1)
            pe.wait_ge(furthest_made, 1)
            nc.tensor.transpose(p_far, furthest, ident).then_inc(furthest_flipped, 1)
            open_counts(0)
            pipeline(pe, PAIRS, RING, [(0, count(0))])
            close_counts()
            pe.wait_ge(weights_loaded, WEIGHT_LOADS)
            for m, name in enumerate(("W0", "W3")):
                nc.tensor.transpose(p_sum[m], bd[name][:, :], ident).then_inc(flipped, 1)
            pe.wait_ge(flip_copied, 1)

            for n in range(5):
                def turn_agg(c, slot, turn, n=n):
                    g = (n - 1) * CHUNKS + c
                    pe.wait_ge(scaled, (n - 1) * CHUNKS + c + 1)
                    wait(pe, agg_T_kept, g if n == 3 else g - 1)
                    dest = p_nT[0 if n == 3 else slot % 2]
                    for j in range(CHUNK // 2):
                        last = nc.tensor.transpose(pair(dest, j), pair(n_a[0][slot % 2], j), ident)
                    if n == 3:
                        for j in range(CHUNK // 2):
                            last = nc.tensor.transpose(pair(p_nT[1], j), pair(n_b, j), ident)
                    last.then_inc(agg_T, 1)

                def product(c, slot, turn, n=n):
                    pe.wait_ge(z_ready if n == 3 else agg_T_kept, (c if n == 3 else (n - 1) * CHUNKS + c) + 1)
                    if n == 1:
                        wait(pe, rectified, c - 1)
                    else:
                        wait(pe, x_part if n == 3 else x_new, (1 if n == 3 else n - 1) * CHUNKS + c - (0 if n == 3 else 1))
                    dest = p_nO[1 if n == 3 else slot % 2]
                    rows_T_ = (n_r if n == 3 else n_T)[slot % 2]
                    for j in range(CHUNK // 2):
                        last = nc.tensor.matmul(pair(dest, j), pair(rows_T_, j),
                                                bd[{1: "W0", 2: "W1", 3: "Wn2", 4: "W3"}[n]][:, :],
                                                start=True, stop=(n == 3))
                        if n != 3:
                            last = nc.tensor.matmul(pair(dest, j), ones[:, :], bias[n - 1][:, :], start=False, stop=True)
                    last.then_inc(agg_out, 1)

                def node_mlp(c, slot, turn):
                    pe.wait_ge(agg_T_kept, 2 * CHUNKS + c + 1)
                    wait(pe, z_ready, c)
                    for lo, hi in ((0, 512), (512, CW)):
                        nc.tensor.matmul(p_nO[0][:, lo:hi], bd["Wn1h"][:, :], n_y[slot % 2][:, lo:hi], start=True, stop=False)
                        last = nc.tensor.matmul(p_nO[0][:, lo:hi], bd["Wn1a"][:, :], n_T[slot % 2][:, lo:hi],
                                                start=False, stop=True)
                    last.then_inc(z_out, 1)

                if n:
                    pipeline(pe, CHUNKS, NRING, [(2, product), (1, node_mlp), (0, turn_agg)] if n == 3 else
                             [(0, turn_agg), (1, product)])
                if n == 4:
                    break
                l = n

                def window_sums(q, slot, turn, l=l):
                    g = KEYED[l] * PAIRS + q
                    pe.wait_ge(gathered[slot], gathers_before[l] + 16 * 2 * (turn + 1))
                    pe.wait_ge(window_hot, g + 1)
                    if not (isinstance(g, int) and g < 2):
                        pe.wait_ge(folded, 2 * (g - 1))
                    for j in range(2):
                        for b in range(WIN):
                            for k in range(3):
                                last = nc.tensor.matmul(
                                    p_win[third[slot]][:, j * WD + b * D:j * WD + (b + 1) * D],
                                    e_win[third[slot]][:, j * WP + b * P:j * WP + (b + 1) * P],
                                    e_parts[slot][:, j * D3 + k * D:j * D3 + (k + 1) * D],
                                    start=(k == 0), stop=(k == 2))
                    last.then_inc(window_summed, 1)

                def stragglers(l=l):
                    w = KEYED[l]
                    with pe.Fori(0, C) as a:
                        g = w * C + a
                        pe.wait_ge(f_ready, g + 1)
                        nc.tensor.transpose(p_key[0][:, 0:P], f_flt[:, 0:1].to_broadcast([P, P]),
                                            ident).then_inc(f_spread, 1)
                        pe.wait_ge(f_gathered, 16 * (g + 1))
                        pe.wait_ge(f_equal, g + 1)
                        for k in range(3):
                            last = nc.tensor.matmul(p_sum[0][:, 0:D], f_eq, f_rows[:, k * D:(k + 1) * D],
                                                    start=(k == 0), stop=(k == 2))
                        last.then_inc(f_summed, 1)

                def spread_key(q, slot, turn):
                    pe.wait_ge(rows_ready, L2 * PAIRS + q + 1)
                    wait(pe, equal, last_use(q, slot))
                    for j in range(2):
                        last = nc.tensor.transpose(p_key[slot % 2][:, j * P:(j + 1) * P],
                                                   e_flt[slot][:, 2 * j:2 * j + 1].to_broadcast([P, P]), ident)
                    last.then_inc(key_spread, 1)

                def add_up(q, slot, turn):
                    pe.wait_ge(weighted, q + 1)
                    pe.wait_ge(equal, q + 1)
                    wait(pe, msg_ready, last_use(q, slot))
                    for j in range(2):
                        last = nc.tensor.matmul(p_sum[slot % 2][:, j * D:(j + 1) * D],
                                                e_eq[slot][:, j * P:(j + 1) * P],
                                                e_raw[slot][:, j * D:(j + 1) * D], start=True, stop=True)
                    last.then_inc(summed, 1)

                def turn_rows(q, slot, turn):
                    pe.wait_ge(gathered[slot], gathers_before[L2] + 16 * 2 * tables_in[L2] * (turn + 1))
                    wait(pe, rows_T, q)
                    for k in range(2):
                        last = nc.tensor.transpose(p_T[:, k * P:(k + 1) * P], e_row[k][slot], ident)
                    last.then_inc(flipped_rows, 1)

                def edge_mlp1(q, slot, turn):
                    pe.wait_ge(rows_T, q + 1)
                    pe.wait_ge(radial_term, q + 1)
                    wait(pe, act1, q)
                    nc.tensor.matmul(p_mlp[0], bd["We1s"][:, :], e_T[slot % 2][:, 0:P], start=True, stop=False)
                    nc.tensor.matmul(p_mlp[0], bd["We1d"][:, :], e_T[slot % 2][:, P:2 * P], start=False, stop=False)
                    nc.tensor.matmul(p_mlp[0], e_X[slot], ident, start=False, stop=True).then_inc(mlp1, 1)

                def edge_mlp2(q, slot, turn):
                    pe.wait_ge(act1, q + 1)
                    wait(pe, act2, q)
                    nc.tensor.matmul(p_mlp[1], bd["We2"][:, :], e_h1[slot % 2], start=True, stop=True).then_inc(mlp2, 1)

                def turn_back(q, slot, turn):
                    pe.wait_ge(act2, q + 1)
                    wait(pe, weighted, q)
                    nc.tensor.matmul(p_nat, e_h2[slot % 2], ext[:, :], start=True, stop=True).then_inc(natural, 1)

                if l == L2:
                    pipeline(pe, PAIRS, RING, [(0, spread_key), (0, turn_rows), (1, edge_mlp2), (0, edge_mlp1),
                                               (1, turn_back), (1, add_up)])
                    continue
                if l == L0:
                    pe.wait_ge(flag_ready, 1)
                    any_missed = pe.value_load(flag[0:1, 0:1], min_val=0, max_val=1)
                    open_counts(1)
                    pipeline(pe, PAIRS, RING, [(0, window_sums), (1, count(1))])
                    close_counts()
                else:
                    pipeline(pe, PAIRS, RING, [(0, window_sums)])
                with pe.If(any_missed > 0):
                    stragglers()


_INS = ['x', 'src', 'dst', 'edge_attr_3', 'L0_gnn_W', 'L0_gnn_b', 'L0_gnn_prelu_a', 'L1_gnn_weight', 'L1_gnn_bias',
        'L2_gnn_We1', 'L2_gnn_be1', 'L2_gnn_We2', 'L2_gnn_be2', 'L2_gnn_Wa', 'L2_gnn_ba', 'L2_gnn_Wn1',
        'L2_gnn_bn1', 'L2_gnn_Wn2', 'L2_gnn_bn2', 'L3_gnn_W', 'L3_gnn_b']


def kernel(**inputs):
    import numpy as _np
    import concourse.bacc as _bacc
    from concourse import mybir as _mybir
    from concourse.bass_utils import run_bass_kernel_spmd as _run

    nc = _bacc.Bacc("TRN2", target_bir_lowering=False, num_devices=1)
    arrays, args = {}, []
    for name in _INS:
        a = _np.ascontiguousarray(inputs[name])
        arrays[f"in_{name}"] = a
        args.append(nc.dram_tensor(f"in_{name}", a.shape, _mybir.dt.from_np(a.dtype), kind="ExternalInput").ap())
    out = nc.dram_tensor("out_x", (N, D), F32, kind="ExternalOutput").ap()
    gnn_kernel(nc, *args, out)
    r = _run(nc, [arrays], core_ids=[0])
    return r.results[0]["out_x"]
```
